# Optimizing a Trainium2 kernel written in Bass

```python
import numpy as np
import jax
import jax.numpy as jnp

def _softmax(x, axis=-1):
    return jax.nn.softmax(x, axis=axis)

def _gelu(x):
    return jax.nn.gelu(x, approximate=True)

def _silu(x):
    return jax.nn.silu(x)

def _sigmoid(x):
    return jax.nn.sigmoid(x)

def _layernorm(x, axis=-1, eps=1e-05):
    m = jnp.mean(x, axis=axis, keepdims=True)
    v = jnp.var(x, axis=axis, keepdims=True)
    return (x - m) / jnp.sqrt(v + eps)

def _scatter_add(tgt, idx, src, axis=0):
    return tgt.at[idx].add(src)

def _segment_sum(src, seg, n):
    return jax.ops.segment_sum(src, seg, n)
kernel_name = 'mk_seq_postln_d2_jaxref_r8_f77dcd'

def setup_inputs(seed: int=0):
    np.random.seed(seed)
    _w = jnp.asarray

    def _L0_attn_setup():
        import jax, jax.numpy as jnp
        import numpy as np
        B, T, D = (1, 256, 128)
        H, DH, DV, DF = (16, 64, 64, 512)
        EPS_LN = 1e-05
        EPS_DEN = 1e-06

        def _layernorm(x, g, b):
            m = jnp.mean(x, axis=-1, keepdims=True)
            v = jnp.mean((x - m) ** 2, axis=-1, keepdims=True)
            return (x - m) / jnp.sqrt(v + EPS_LN) * g + b

        def _phi(x):
            return jax.nn.elu(x) + 1.0

        def _linear_attention(x, Wq, Wk, Wv, Wo):
            b, t, d = x.shape
            Q = _phi((x @ Wq).reshape(b, t, H, DH)).transpose(0, 2, 1, 3)
            K = _phi((x @ Wk).reshape(b, t, H, DH)).transpose(0, 2, 1, 3)
            V = (x @ Wv).reshape(b, t, H, DV).transpose(0, 2, 1, 3)
            KV = jnp.einsum('bhti,bhtj->bhtij', K, V)
            S = jnp.cumsum(KV, axis=2)
            z = jnp.cumsum(K, axis=2)
            num = jnp.einsum('bhti,bhtij->bhtj', Q, S)
            den = jnp.maximum(jnp.einsum('bhti,bhti->bht', Q, z), EPS_DEN)[..., None]
            out = (num / den).transpose(0, 2, 1, 3).reshape(b, t, H * DV)
            return out @ Wo
        key = jax.random.key(seed)
        ks = jax.random.split(key, 8)
        s = 0.02
        return {'x': jax.random.normal(ks[0], (B, T, D), dtype=jnp.float32), 'ln1_g': jnp.ones((D,), jnp.float32), 'ln1_b': jnp.zeros((D,), jnp.float32), 'Wq': jax.random.normal(ks[1], (D, H * DH), jnp.float32) * s, 'Wk': jax.random.normal(ks[2], (D, H * DH), jnp.float32) * s, 'Wv': jax.random.normal(ks[3], (D, H * DV), jnp.float32) * s, 'Wo': jax.random.normal(ks[4], (H * DV, D), jnp.float32) * s, 'ln2_g': jnp.ones((D,), jnp.float32), 'ln2_b': jnp.zeros((D,), jnp.float32), 'Wf1': jax.random.normal(ks[5], (D, DF), jnp.float32) * s, 'Wf2': jax.random.normal(ks[6], (DF, D), jnp.float32) * s}
    _L0_attn_in = _L0_attn_setup()

    def _L0_ffn_setup():
        import jax, jax.numpy as jnp
        import numpy as np
        LN_EPS = 1e-05

        def layer_norm(x, g, b):
            mu = jnp.mean(x, axis=-1, keepdims=True)
            var = jnp.mean(jnp.square(x - mu), axis=-1, keepdims=True)
            return (x - mu) * jax.lax.rsqrt(var + LN_EPS) * g + b

        def ternary_quant(w):
            scale = 1.0 / jnp.clip(jnp.mean(jnp.abs(w)), 1e-05)
            wq = jnp.clip(jnp.round(w * scale), -1.0, 1.0) / scale
            return w + jax.lax.stop_gradient(wq - w)
        key = jax.random.key(seed)
        ks = jax.random.split(key, 3)
        dim, hidden = (128, 512)
        B, S = (8, 128)
        x = jax.random.normal(ks[0], (B, S, dim), dtype=jnp.float32)
        w1 = jax.random.normal(ks[1], (hidden, dim), dtype=jnp.float32) * 0.02
        w2 = jax.random.normal(ks[2], (dim, hidden), dtype=jnp.float32) * 0.02
        return {'x': x, 'ln1_g': jnp.ones((dim,), jnp.float32), 'ln1_b': jnp.zeros((dim,), jnp.float32), 'w1': w1, 'b1': jnp.zeros((hidden,), jnp.float32), 'ln2_g': jnp.ones((hidden,), jnp.float32), 'ln2_b': jnp.zeros((hidden,), jnp.float32), 'w2': w2, 'b2': jnp.zeros((dim,), jnp.float32)}
    _L0_ffn_in = _L0_ffn_setup()

    def _L1_attn_setup():
        import jax, jax.numpy as jnp
        import numpy as np
        D_MODEL = 128
        N_HEADS = 4
        N_KV_HEADS = 2
        HEAD_DIM = D_MODEL // N_HEADS
        N_REP = N_HEADS // N_KV_HEADS
        EPS_RMS = 1e-06
        EPS_NORM = 1e-12

        def _rmsnorm(x, w):
            var = jnp.mean(jnp.square(x), axis=-1, keepdims=True)
            return x * jax.lax.rsqrt(var + EPS_RMS) * w

        def _l2norm(x):
            n = jnp.sqrt(jnp.sum(jnp.square(x), axis=-1, keepdims=True))
            return x / jnp.maximum(n, EPS_NORM)
        key = jax.random.key(seed)
        ks = jax.random.split(key, 8)
        B, L = (2, 512)
        s = 0.02
        return {'x': jax.random.normal(ks[0], (B, L, D_MODEL), dtype=jnp.float32), 'norm_w': jnp.ones((D_MODEL,), dtype=jnp.float32), 'Wq': jax.random.normal(ks[1], (D_MODEL, N_HEADS * HEAD_DIM), dtype=jnp.float32) * s, 'Wk': jax.random.normal(ks[2], (D_MODEL, N_KV_HEADS * HEAD_DIM), dtype=jnp.float32) * s, 'Wv': jax.random.normal(ks[3], (D_MODEL, N_KV_HEADS * HEAD_DIM), dtype=jnp.float32) * s, 'Wo': jax.random.normal(ks[4], (N_HEADS * HEAD_DIM, D_MODEL), dtype=jnp.float32) * s, 'gate': jnp.asarray(0.1, dtype=jnp.float32), 'log_temperature': jnp.asarray(np.log(10.0), dtype=jnp.float32)}
    _L1_attn_in = _L1_attn_setup()

    def _L1_ffn_setup():
        import jax, jax.numpy as jnp
        import numpy as np
        LATENT = 128
        LEAF_W = 64
        DEPTH = 4
        N_LEAVES = 2 ** DEPTH
        N_NODES = 2 ** DEPTH - 1
        B, S = (4, 256)

        def _fff_params(key, prefix):
            ks = jax.random.split(key, 4)
            d, h, l, n = (LATENT, LEAF_W, N_LEAVES, N_NODES)
            s_in = 1.0 / np.sqrt(d).astype(np.float32)
            s_h = 1.0 / np.sqrt(h).astype(np.float32)
            return {f'{prefix}_node_w': jax.random.normal(ks[0], (n, d), jnp.float32) * s_in, f'{prefix}_node_b': jax.random.normal(ks[1], (n,), jnp.float32) * s_in, f'{prefix}_w1': jax.random.normal(ks[2], (l, d, h), jnp.float32) * s_in, f'{prefix}_b1': jnp.zeros((l, h), jnp.float32), f'{prefix}_w2': jax.random.normal(ks[3], (l, h, d), jnp.float32) * s_h, f'{prefix}_b2': jnp.zeros((l, d), jnp.float32)}

        def _fff(x, node_w, node_b, w1, b1, w2, b2):
            Bx, Sx, D = x.shape
            xf = x.reshape(-1, D)
            N = xf.shape[0]
            cur = jnp.zeros((N,), jnp.int32)
            for _ in range(DEPTH):
                pw = node_w[cur]
                score = jnp.einsum('nd,nd->n', xf, pw) + node_b[cur]
                cur = 2 * cur + 1 + (score >= 0).astype(jnp.int32)
            leaf = cur - N_NODES
            sel = jax.nn.one_hot(leaf, N_LEAVES, dtype=xf.dtype)
            hidden_all = jax.nn.relu(jnp.einsum('nd,ldh->lnh', xf, w1) + b1[:, None, :])
            hidden = hidden_all * sel.T[:, :, None]
            out = jnp.einsum('lnh,lho->no', hidden, w2) + sel @ b2
            return out.reshape(Bx, Sx, D)
        key = jax.random.key(seed)
        kx, kq, kk, kv = jax.random.split(key, 4)
        inp = {'x': jax.random.normal(kx, (B, S, LATENT), jnp.float32)}
        inp.update(_fff_params(kq, 'q'))
        inp.update(_fff_params(kk, 'k'))
        inp.update(_fff_params(kv, 'v'))
        return inp
    _L1_ffn_in = _L1_ffn_setup()
    _d = {'L0_attn_x': _L0_attn_in['x'], 'L0_attn_ln1_g': _L0_attn_in['ln1_g'], 'L0_attn_ln1_b': _L0_attn_in['ln1_b'], 'L0_attn_Wq': _L0_attn_in['Wq'], 'L0_attn_Wk': _L0_attn_in['Wk'], 'L0_attn_Wv': _L0_attn_in['Wv'], 'L0_attn_Wo': _L0_attn_in['Wo'], 'L0_attn_ln2_g': _L0_attn_in['ln2_g'], 'L0_attn_ln2_b': _L0_attn_in['ln2_b'], 'L0_attn_Wf1': _L0_attn_in['Wf1'], 'L0_attn_Wf2': _L0_attn_in['Wf2'], 'L0_ffn_ln1_g': _L0_ffn_in['ln1_g'], 'L0_ffn_ln1_b': _L0_ffn_in['ln1_b'], 'L0_ffn_w1': _L0_ffn_in['w1'], 'L0_ffn_b1': _L0_ffn_in['b1'], 'L0_ffn_ln2_g': _L0_ffn_in['ln2_g'], 'L0_ffn_ln2_b': _L0_ffn_in['ln2_b'], 'L0_ffn_w2': _L0_ffn_in['w2'], 'L0_ffn_b2': _L0_ffn_in['b2'], 'L1_attn_norm_w': _L1_attn_in['norm_w'], 'L1_attn_Wq': _L1_attn_in['Wq'], 'L1_attn_Wk': _L1_attn_in['Wk'], 'L1_attn_Wv': _L1_attn_in['Wv'], 'L1_attn_Wo': _L1_attn_in['Wo'], 'L1_attn_gate': _L1_attn_in['gate'], 'L1_attn_log_temperature': _L1_attn_in['log_temperature'], 'L1_ffn_q_node_w': _L1_ffn_in['q_node_w'], 'L1_ffn_q_node_b': _L1_ffn_in['q_node_b'], 'L1_ffn_q_w1': _L1_ffn_in['q_w1'], 'L1_ffn_q_b1': _L1_ffn_in['q_b1'], 'L1_ffn_q_w2': _L1_ffn_in['q_w2'], 'L1_ffn_q_b2': _L1_ffn_in['q_b2'], 'L1_ffn_k_node_w': _L1_ffn_in['k_node_w'], 'L1_ffn_k_node_b': _L1_ffn_in['k_node_b'], 'L1_ffn_k_w1': _L1_ffn_in['k_w1'], 'L1_ffn_k_b1': _L1_ffn_in['k_b1'], 'L1_ffn_k_w2': _L1_ffn_in['k_w2'], 'L1_ffn_k_b2': _L1_ffn_in['k_b2'], 'L1_ffn_v_node_w': _L1_ffn_in['v_node_w'], 'L1_ffn_v_node_b': _L1_ffn_in['v_node_b'], 'L1_ffn_v_w1': _L1_ffn_in['v_w1'], 'L1_ffn_v_b1': _L1_ffn_in['v_b1'], 'L1_ffn_v_w2': _L1_ffn_in['v_w2'], 'L1_ffn_v_b2': _L1_ffn_in['v_b2']}
    _x0 = _d['L0_attn_x']
    _d['L0_attn_x'] = jax.random.normal(jax.random.fold_in(jax.random.key(seed), 1), (8, 1024, 128), dtype=_x0.dtype)
    del _x0
    return _d

def reference(L0_attn_x, L0_attn_ln1_g, L0_attn_ln1_b, L0_attn_Wq, L0_attn_Wk, L0_attn_Wv, L0_attn_Wo, L0_attn_ln2_g, L0_attn_ln2_b, L0_attn_Wf1, L0_attn_Wf2, L0_ffn_ln1_g, L0_ffn_ln1_b, L0_ffn_w1, L0_ffn_b1, L0_ffn_ln2_g, L0_ffn_ln2_b, L0_ffn_w2, L0_ffn_b2, L1_attn_norm_w, L1_attn_Wq, L1_attn_Wk, L1_attn_Wv, L1_attn_Wo, L1_attn_gate, L1_attn_log_temperature, L1_ffn_q_node_w, L1_ffn_q_node_b, L1_ffn_q_w1, L1_ffn_q_b1, L1_ffn_q_w2, L1_ffn_q_b2, L1_ffn_k_node_w, L1_ffn_k_node_b, L1_ffn_k_w1, L1_ffn_k_b1, L1_ffn_k_w2, L1_ffn_k_b2, L1_ffn_v_node_w, L1_ffn_v_node_b, L1_ffn_v_w1, L1_ffn_v_b1, L1_ffn_v_w2, L1_ffn_v_b2):

    def _L0_attn_ref(x, ln1_g, ln1_b, Wq, Wk, Wv, Wo, ln2_g, ln2_b, Wf1, Wf2):
        import jax, jax.numpy as jnp
        import numpy as np
        B, T, D = (1, 256, 128)
        H, DH, DV, DF = (16, 64, 64, 512)
        EPS_LN = 1e-05
        EPS_DEN = 1e-06

        def _layernorm(x, g, b):
            m = jnp.mean(x, axis=-1, keepdims=True)
            v = jnp.mean((x - m) ** 2, axis=-1, keepdims=True)
            return (x - m) / jnp.sqrt(v + EPS_LN) * g + b

        def _phi(x):
            return jax.nn.elu(x) + 1.0

        def _linear_attention(x, Wq, Wk, Wv, Wo):
            b, t, d = x.shape
            Q = _phi((x @ Wq).reshape(b, t, H, DH)).transpose(0, 2, 1, 3)
            K = _phi((x @ Wk).reshape(b, t, H, DH)).transpose(0, 2, 1, 3)
            V = (x @ Wv).reshape(b, t, H, DV).transpose(0, 2, 1, 3)
            KV = jnp.einsum('bhti,bhtj->bhtij', K, V)
            S = jnp.cumsum(KV, axis=2)
            z = jnp.cumsum(K, axis=2)
            num = jnp.einsum('bhti,bhtij->bhtj', Q, S)
            den = jnp.maximum(jnp.einsum('bhti,bhti->bht', Q, z), EPS_DEN)[..., None]
            out = (num / den).transpose(0, 2, 1, 3).reshape(b, t, H * DV)
            return out @ Wo
        x = x + _linear_attention(_layernorm(x, ln1_g, ln1_b), Wq, Wk, Wv, Wo)
        h = _layernorm(x, ln2_g, ln2_b)
        x = x + jax.nn.gelu(h @ Wf1, approximate=False) @ Wf2
        return x

    def _L0_ffn_ref(x, ln1_g, ln1_b, w1, b1, ln2_g, ln2_b, w2, b2):
        import jax, jax.numpy as jnp
        import numpy as np
        LN_EPS = 1e-05

        def layer_norm(x, g, b):
            mu = jnp.mean(x, axis=-1, keepdims=True)
            var = jnp.mean(jnp.square(x - mu), axis=-1, keepdims=True)
            return (x - mu) * jax.lax.rsqrt(var + LN_EPS) * g + b

        def ternary_quant(w):
            scale = 1.0 / jnp.clip(jnp.mean(jnp.abs(w)), 1e-05)
            wq = jnp.clip(jnp.round(w * scale), -1.0, 1.0) / scale
            return w + jax.lax.stop_gradient(wq - w)
        h = layer_norm(x, ln1_g, ln1_b)
        h = jnp.einsum('bsd,hd->bsh', h, ternary_quant(w1)) + b1
        h = jax.nn.gelu(h, approximate=False)
        h = layer_norm(h, ln2_g, ln2_b)
        out = jnp.einsum('bsh,dh->bsd', h, ternary_quant(w2)) + b2
        return out

    def _L1_attn_ref(x, norm_w, Wq, Wk, Wv, Wo, gate, log_temperature):
        import jax, jax.numpy as jnp
        import numpy as np
        D_MODEL = 128
        N_HEADS = 4
        N_KV_HEADS = 2
        HEAD_DIM = D_MODEL // N_HEADS
        N_REP = N_HEADS // N_KV_HEADS
        EPS_RMS = 1e-06
        EPS_NORM = 1e-12

        def _rmsnorm(x, w):
            var = jnp.mean(jnp.square(x), axis=-1, keepdims=True)
            return x * jax.lax.rsqrt(var + EPS_RMS) * w

        def _l2norm(x):
            n = jnp.sqrt(jnp.sum(jnp.square(x), axis=-1, keepdims=True))
            return x / jnp.maximum(n, EPS_NORM)
        B, L, D = x.shape
        h = _rmsnorm(x, norm_w)
        q = (h @ Wq).reshape(B, L, N_HEADS, HEAD_DIM).transpose(0, 2, 1, 3)
        k = (h @ Wk).reshape(B, L, N_KV_HEADS, HEAD_DIM).transpose(0, 2, 1, 3)
        v = (h @ Wv).reshape(B, L, N_KV_HEADS, HEAD_DIM).transpose(0, 2, 1, 3)
        if N_REP > 1:
            k = jnp.repeat(k, N_REP, axis=1)
            v = jnp.repeat(v, N_REP, axis=1)
        q = _l2norm(q)
        k = _l2norm(k)
        scale = jnp.exp(log_temperature)
        attn = jnp.einsum('bhqd,bhkd->bhqk', q, k) * scale
        causal = jnp.tril(jnp.ones((L, L), dtype=bool))
        attn = jnp.where(causal, attn, -jnp.inf)
        attn = jax.nn.softmax(attn, axis=-1)
        out = jnp.einsum('bhqk,bhkd->bhqd', attn, v).transpose(0, 2, 1, 3).reshape(B, L, D)
        out = out @ Wo
        return x + gate * out

    def _L1_ffn_ref(x, q_node_w, q_node_b, q_w1, q_b1, q_w2, q_b2, k_node_w, k_node_b, k_w1, k_b1, k_w2, k_b2, v_node_w, v_node_b, v_w1, v_b1, v_w2, v_b2):
        import jax, jax.numpy as jnp
        import numpy as np
        LATENT = 128
        LEAF_W = 64
        DEPTH = 4
        N_LEAVES = 2 ** DEPTH
        N_NODES = 2 ** DEPTH - 1
        B, S = (4, 256)

        def _fff_params(key, prefix):
            ks = jax.random.split(key, 4)
            d, h, l, n = (LATENT, LEAF_W, N_LEAVES, N_NODES)
            s_in = 1.0 / np.sqrt(d).astype(np.float32)
            s_h = 1.0 / np.sqrt(h).astype(np.float32)
            return {f'{prefix}_node_w': jax.random.normal(ks[0], (n, d), jnp.float32) * s_in, f'{prefix}_node_b': jax.random.normal(ks[1], (n,), jnp.float32) * s_in, f'{prefix}_w1': jax.random.normal(ks[2], (l, d, h), jnp.float32) * s_in, f'{prefix}_b1': jnp.zeros((l, h), jnp.float32), f'{prefix}_w2': jax.random.normal(ks[3], (l, h, d), jnp.float32) * s_h, f'{prefix}_b2': jnp.zeros((l, d), jnp.float32)}

        def _fff(x, node_w, node_b, w1, b1, w2, b2):
            Bx, Sx, D = x.shape
            xf = x.reshape(-1, D)
            N = xf.shape[0]
            cur = jnp.zeros((N,), jnp.int32)
            for _ in range(DEPTH):
                pw = node_w[cur]
                score = jnp.einsum('nd,nd->n', xf, pw) + node_b[cur]
                cur = 2 * cur + 1 + (score >= 0).astype(jnp.int32)
            leaf = cur - N_NODES
            sel = jax.nn.one_hot(leaf, N_LEAVES, dtype=xf.dtype)
            hidden_all = jax.nn.relu(jnp.einsum('nd,ldh->lnh', xf, w1) + b1[:, None, :])
            hidden = hidden_all * sel.T[:, :, None]
            out = jnp.einsum('lnh,lho->no', hidden, w2) + sel @ b2
            return out.reshape(Bx, Sx, D)
        q = _fff(x, q_node_w, q_node_b, q_w1, q_b1, q_w2, q_b2)
        k = _fff(x, k_node_w, k_node_b, k_w1, k_b1, k_w2, k_b2)
        v = _fff(x, v_node_w, v_node_b, v_w1, v_b1, v_w2, v_b2)
        scale = 1.0 / np.sqrt(LATENT).astype(np.float32)
        attn = jax.nn.softmax(jnp.einsum('bqd,bkd->bqk', q, k) * scale, axis=-1)
        return jnp.einsum('bqk,bkd->bqd', attn, v)
    x = L0_attn_x
    x = _layernorm(x + _L0_attn_ref(x, L0_attn_ln1_g, L0_attn_ln1_b, L0_attn_Wq, L0_attn_Wk, L0_attn_Wv, L0_attn_Wo, L0_attn_ln2_g, L0_attn_ln2_b, L0_attn_Wf1, L0_attn_Wf2), axis=-1)
    x = _layernorm(x + _L0_ffn_ref(x, L0_ffn_ln1_g, L0_ffn_ln1_b, L0_ffn_w1, L0_ffn_b1, L0_ffn_ln2_g, L0_ffn_ln2_b, L0_ffn_w2, L0_ffn_b2), axis=-1)
    x = _layernorm(x + _L1_attn_ref(x, L1_attn_norm_w, L1_attn_Wq, L1_attn_Wk, L1_attn_Wv, L1_attn_Wo, L1_attn_gate, L1_attn_log_temperature), axis=-1)
    x = _layernorm(x + _L1_ffn_ref(x, L1_ffn_q_node_w, L1_ffn_q_node_b, L1_ffn_q_w1, L1_ffn_q_b1, L1_ffn_q_w2, L1_ffn_q_b2, L1_ffn_k_node_w, L1_ffn_k_node_b, L1_ffn_k_w1, L1_ffn_k_b1, L1_ffn_k_w2, L1_ffn_k_b2, L1_ffn_v_node_w, L1_ffn_v_node_b, L1_ffn_v_w1, L1_ffn_v_b1, L1_ffn_v_w2, L1_ffn_v_b2), axis=-1)
    return x

_drawn_inputs = setup_inputs


def setup_inputs(seed=0):
    import zlib

    import numpy as np

    out = dict(_drawn_inputs(seed))
    spreads = {'L0_attn_ln1_g': (1.0, 0.6),
     'L0_attn_ln1_b': (0.0, 0.8),
     'L0_attn_ln2_g': (1.0, 0.6),
     'L0_attn_ln2_b': (0.0, 0.8),
     'L0_ffn_ln1_g': (1.0, 0.2),
     'L0_ffn_ln1_b': (0.0, 0.299),
     'L0_ffn_b1': (0.0, 0.1),
     'L0_ffn_ln2_g': (1.0, 0.2),
     'L0_ffn_ln2_b': (0.0, 0.281),
     'L0_ffn_b2': (0.0, 0.1),
     'L1_attn_norm_w': (1.0, 0.6),
     'L1_ffn_q_b1': (0.0, 0.8),
     'L1_ffn_q_b2': (0.0, 0.8),
     'L1_ffn_k_b1': (0.0, 0.8),
     'L1_ffn_k_b2': (0.0, 0.8),
     'L1_ffn_v_b1': (0.0, 0.556),
     'L1_ffn_v_b2': (0.0, 0.31)}
    factors = {'L0_attn_Wq': 8.0,
     'L0_attn_Wk': 8.0,
     'L0_attn_Wv': 5.437,
     'L0_attn_Wo': 5.54,
     'L1_attn_Wq': 8.0,
     'L1_attn_Wk': 8.0,
     'L1_attn_Wv': 8.0,
     'L1_attn_Wo': 8.0,
     'L1_ffn_q_node_w': 4.62,
     'L1_ffn_q_node_b': 8.0,
     'L1_ffn_q_w1': 5.461,
     'L1_ffn_q_w2': 4.49,
     'L1_ffn_k_node_w': 4.523,
     'L1_ffn_k_node_b': 8.0,
     'L1_ffn_k_w1': 5.297,
     'L1_ffn_k_w2': 4.44,
     'L1_ffn_v_node_b': 2.734}
    for name, (base, spread) in spreads.items():
        noise = np.random.default_rng([zlib.crc32(name.encode()), seed]).standard_normal(out[name].shape)
        drawn = base * np.exp(spread * noise) if base else spread * noise
        out[name] = jnp.asarray(drawn.astype(out[name].dtype))
    for name, factor in factors.items():
        out[name] = (out[name] * factor).astype(out[name].dtype)
    return out
```

```python
from contextlib import ExitStack

import numpy as np

import concourse.bass as bass
from concourse import mybir

F32 = mybir.dt.float32
F32R = mybir.dt.float32r
BF16 = mybir.dt.bfloat16
I32 = mybir.dt.int32
ALU = mybir.AluOpType
ACT = mybir.ActivationFunctionType
AX = mybir.AxisListType

P = 128
NBANK = 8
PRIMED = 1


class Groups:

    def __init__(self, names, before, undrained=(0,) * NBANK, held=(), held_banks=()):
        self.undrained = undrained
        self.slot, count = {}, [0] * NBANK
        rings = {False: [k for k in range(NBANK) if k not in held_banks], True: list(held_banks)}
        turn = {False: 0, True: 0}
        for name in names:
            own = name[0] in held
            k = rings[own][turn[own] % len(rings[own])]
            turn[own] += 1
            self.slot[name] = (k, count[k])
            count[k] += 1
        self.before, self.per = list(before), count

    def after(self, rounds):
        return [b + rounds * p for b, p in zip(self.before, self.per)]

    def filled(self, name, i):
        k, u = self.slot[name]
        return i * self.per[k] + (self.before[k] + u + 1)

    def free(self, name, i):
        k, u = self.slot[name]
        return i * self.per[k] + (self.before[k] - self.undrained[k] + u + PRIMED)

    def drained(self, name, i):
        return self.free(name, i) + 1


def build(nc, t):
    ctx = ExitStack()
    with ctx:
        bank = [ctx.enter_context(nc.psum_tensor(f"bank{k}", [P, 512], F32)) for k in range(NBANK)]
        filled = [ctx.enter_context(nc.semaphore(f"filled{k}")) for k in range(NBANK)]
        drained = [ctx.enter_context(nc.semaphore(f"drained{k}")) for k in range(NBANK)]
        ident = ctx.enter_context(nc.sbuf_tensor("ident", [P, P], F32))
        last = phase_a(nc, t, ctx, bank, filled, drained, ident)
        phase_b(nc, t, ctx, bank, filled, drained, last, ident)


RSQRT_STEPS = 10


def rsqrt_steps(dve, y, u, x):
    return [lambda: dve.tensor_scalar(u.bitcast(I32), x.bitcast(I32), 1, None, ALU.logical_shift_right),
            lambda: dve.tensor_scalar(y.bitcast(I32), u.bitcast(I32), -1.0, float(0x5F1FFFF9), ALU.mult, ALU.add),
            lambda: dve.tensor_tensor(u, y, y, ALU.mult),
            lambda: dve.scalar_tensor_tensor(u, u, -0.703952253, x, ALU.mult, ALU.mult),
            lambda: dve.scalar_tensor_tensor(y, u, 0.703952253 * 2.38924456, y, ALU.add, ALU.mult),
            lambda: dve.tensor_tensor(u, y, y, ALU.mult),
            lambda: dve.tensor_tensor(u, u, x, ALU.mult),
            lambda: dve.scalar_tensor_tensor(u, u, -10.0 / 3.0, u, ALU.add, ALU.mult),
            lambda: dve.tensor_scalar(u, u, 0.375, 1.875, ALU.mult, ALU.add),
            lambda: dve.tensor_tensor(y, y, u, ALU.mult)]


def round_of_phase_a(NM, NF, NS, NQ, PAIRS):
    steps = [("wo",)]
    steps += [(kind, m) for kind in "qk" for m in range(NM)]
    for n in range(NS * NQ + 4):
        if n == 0:
            steps += [("kt", 0, h) for h in range(2)]
        if n % NQ == 0 and n < NS * NQ:
            steps.append(("kbd", n // NQ))
        if n % NQ == 2 and n // NQ + 1 < NS:
            steps += [(kind, n // NQ + 1, h) for kind in ("v", "kt")[n < NQ:] for h in range(2)]
        if n < NS * NQ:
            steps.append(("sc", n))
        if 0 <= n - 2 < NS * NQ:
            steps.append(("av", n - 2))
            if (n - 2) % NQ == NQ - 1:
                steps += [("st", (n - 2) // NQ, r) for r in range(len(PAIRS))]
        if 0 <= n - 4 and (n - 4) % 2 == 1:
            steps.append(("tr", (n - 4) // 2))
    steps.append(("x1T",))
    tail = {("q", 2): [("v", 0, 0)], ("q", 4): [("v", 0, 1)], ("q", 6): [("v", 1, 0)], ("k", 0): [("v", 1, 1)],
            ("k", 2): [("x2T",)], ("k", 7): [("f1", m) for m in range(NF)], ("sc", 1): [("f2",)],
            ("sc", 7): [("x3T",)], ("sc", 8): [("w1", 0), ("w1", 1)], ("sc", 9): [("w1", 2), ("w1", 3)],
            ("sc", 12): [("hT", m) for m in range(NF)], ("sc", 13): [("w2",)]}
    out = []
    for st in steps:
        out.append(st)
        out += tail.get(st, [])
    return out


def phase_a(nc, t, ctx, bank, filled, drained, ident):
    NB, T, D = t["L0_attn_x"].shape
    H, DH, NS = 16, 64, 4
    HF = t["L0_attn_Wf1"].shape[1]
    NC, NG, NM, NF, NQ = T // P, NB // NS, H * DH // P, HF // P, H // 4
    N = NS * P
    W = DH + 1
    ROUND = 12582912.0
    PAIRS = [(0, 3), (3, 6), (6, 8)]
    ROUNDS = NG * NC
    steps = round_of_phase_a(NM, NF, NS, NQ, PAIRS)
    blocks = [(kind, m) for kind in "qk" for m in range(NM)]
    TAIL = ("wo", "x2T", "f1", "f2", "x3T", "w1", "hT", "w2")
    NOBANK = ("kbd",)
    KBD_ORDER = [(0, 0), (1, 0), (0, 1), (1, 1)] + [(s, half) for s in range(2, NS) for half in range(2)]
    setup = Groups([("wsum", 0), ("wsum", 1), ("wT", 0), ("wT", 1)], [0] * NBANK)
    first = Groups([("x1T",)], setup.after(1), setup.after(1))
    body = Groups([st for st in steps if st[0] not in NOBANK], first.after(1), setup.after(1))
    final = Groups([st for st in steps if st[0] in TAIL], body.after(ROUNDS), setup.after(1))

    with ExitStack() as stack:
        sb = lambda name, shape, dt=F32: stack.enter_context(nc.sbuf_tensor(name, shape, dt))
        sem = lambda name: ctx.enter_context(nc.semaphore(name))

        mask = sb("mask", [P, P])
        ones = sb("ones", [P, P])
        whi = sb("whi", [P, 3, H * DH], F32R)
        wlo = sb("wlo", [P, 3, H * DH], F32R)
        wo = sb("wo", [P, NM, D])
        wf1 = sb("wf1", [P, HF])
        wf2 = sb("wf2", [P, NF, D])
        w1T = sb("w1T", [P, HF])
        w2T = sb("w2T", [P, NF, D])
        lng = sb("lng", [P, 6])
        hln = sb("hln", [P, 2, NF])
        b1r = sb("b1r", [P, HF])
        b2r = sb("b2r", [P, D])

        xs = sb("xs", [P, NS, D])
        xr = sb("xr", [P, NS, D])
        xn = sb("xn", [P, NS, D])
        hT = sb("hT", [P, N])
        hhi = sb("hhi", [P, N], F32R)
        hlo = sb("hlo", [P, N], F32R)
        tmp = sb("tmp", [P, 4, N])
        QT = sb("QT", [P, NM, N])
        KT = sb("KT", [P, NM, N])
        KBD = sb("KBD", [P, 2, NM, 2, P])
        Ktok = sb("Ktok", [P, 2, H * DH])
        V = sb("V", [P, 2, NM, 2, 2 * W])
        S = sb("S", [P, NS, NM, 2 * W])
        PT = sb("PT", [P, 4, 4, P])
        AO = sb("AO", [P, 2, H * DH])
        rden = sb("rden", [P, 4, 4])

        x1 = sb("x1", [P, NS, D])
        x01 = sb("x01", [P, NS, D])
        xn2 = sb("xn2", [P, NS, D])
        xa = sb("xa", [P, NS, D])
        xo = sb("xo", [P, NS, D])
        hT2 = sb("hT2", [P, N])
        GT = sb("GT", [P, NF, N])
        hb = sb("hb", [P, NS, HF])
        bst = sb("bst", [P, 2, NS, 6])
        mv = sb("mv", [P, 2, NS, 2])
        rs = sb("rs", [P, 2, 4, NS])
        pad = sb("pad", [P, 1])
        prime = sb("prime", [P, NBANK + 2])

        w1raw, w2raw = hb[:, 0, :], hb[:, 1, :]
        wabs = rs[:, 1, 3, 0:4]
        wqkv_raw = QT[:, :, :].rearrange("p m n -> p (m n)")[:, 0:3 * H * DH].rearrange("p (w n) -> p w n", w=3)

        w_loaded, w2_loaded = sem("w_loaded"), sem("w2_loaded")
        wabs_ready, wq_ready, wT_ready = sem("wabs_ready"), sem("wq_ready"), sem("wT_ready")
        zeroed, split_w = sem("zeroed"), sem("split_w")
        x_loaded, x_used = sem("x_loaded"), sem("x_used")
        xn_ready, xn2_ready = sem("xn_ready"), sem("xn2_ready")
        hhi_ready, hlo_ready = sem("hhi_ready"), sem("hlo_ready")
        exp_ready, phi_ready = sem("exp_ready"), sem("phi_ready")
        kbd_ready = sem("kbd_ready")
        x01_ready = sem("x01_ready")
        state_ready = sem("state_ready")
        hact_ready, hn_ready = sem("hact_ready"), sem("hn_ready")
        xo_ready, xo_stored, xo_free = sem("xo_ready"), sem("xo_stored"), sem("xo_free")
        dve_step = sem("dve_step")

        block = stack.enter_context(nc.Block())

        def tile_of(ap, g, c):
            return ap.rearrange("b (c p) d -> p b c d", p=P)[:, bass.ds(g * NS, NS), bass.ds(c, 1), :] \
                .rearrange("p b c d -> p (b c) d")

        @block.sync
        def _(sp):
            for dst, src in ((w1raw.rearrange("p (m d) -> p m d", m=NF), t["L0_ffn_w1"].rearrange("(m p) d -> p m d", p=P)),
                             (w2raw, t["L0_ffn_w2"]), (ident[:, :], t["c_ident"]), (mask[:, :], t["c_mask"])):
                sp.dma_start(dst, src).then_inc(w_loaded, 16)
            for n, name in enumerate(("L0_attn_Wq", "L0_attn_Wk", "L0_attn_Wv")):
                sp.dma_start(wqkv_raw[:, n, :], t[name]).then_inc(w2_loaded, 16)
            for n, name in enumerate(("L0_attn_ln1_g", "L0_attn_ln1_b", "L0_attn_ln2_g", "L0_attn_ln2_b", "L0_ffn_ln1_g", "L0_ffn_ln1_b")):
                sp.dma_start(lng[:, n:n + 1], t[name].rearrange("(p a) -> p a", a=1)).then_inc(w2_loaded, 16)
            for n, name in enumerate(("L0_ffn_ln2_g", "L0_ffn_ln2_b")):
                for m in range(NF):
                    sp.dma_start(hln[:, n, m:m + 1], t[name][m * P:(m + 1) * P].rearrange("(p a) -> p a", a=1)).then_inc(w2_loaded, 16)
            sp.dma_start(wo[:, :, :], t["L0_attn_Wo"].rearrange("(m p) d -> p m d", p=P)).then_inc(w2_loaded, 16)
            sp.dma_start(wf1[:, :], t["L0_attn_Wf1"]).then_inc(w2_loaded, 16)
            sp.dma_start(wf2[:, :, :], t["L0_attn_Wf2"].rearrange("(m p) d -> p m d", p=P)).then_inc(w2_loaded, 16)
            sp.dma_start(b1r[:, :], t["L0_ffn_b1"].rearrange("(a n) -> a n", a=1).broadcast_to([P, HF])).then_inc(w2_loaded, 16)
            sp.dma_start(b2r[:, :], t["L0_ffn_b2"].rearrange("(a n) -> a n", a=1).broadcast_to([P, D])).then_inc(w2_loaded, 16)
            with sp.Fori(0, NG) as g:
                with sp.Fori(0, NC) as c:
                    i = g * NC + c
                    sp.wait_ge(x_used, i + PRIMED)
                    sp.dma_start(xs[:, :, :], tile_of(t["L0_attn_x"], g, c)).then_inc(x_loaded, 16)
            sp.wait_ge(x_used, ROUNDS + PRIMED)
            sp.dma_start(xs[:, :, :], tile_of(t["L0_attn_x"], 0, 0)).then_inc(x_loaded, 16)
        W2_DMAS = 3 + 6 + 2 * NF + 3 + 2

        @block.gpsimd
        def _(pool):
            for n, primed in enumerate(drained + [x_used, xo_free]):
                pool.memset(prime[:, n:n + 1], 0.0).then_inc(primed, PRIMED)
            pool.memset(ones[:, :], 1.0).then_inc(zeroed, 1)
            pool.memset(KBD[:, :, :, :, :], 0.0).then_inc(zeroed, 1)
            pool.memset(S[:, :, :, :], 0.0).then_inc(zeroed, 1)
            pool.memset(xr[:, :, :], 0.0).then_inc(zeroed, 1)
            pool.memset(V[:, :, :, 0, W:2 * W], 0.0).then_inc(zeroed, 1)
            pool.memset(V[:, :, :, 1, 0:W], 0.0).then_inc(zeroed, 1)
            pool.memset(V[:, :, :, 0, DH:W], 1.0).then_inc(zeroed, 1)
            pool.memset(V[:, :, :, 1, 2 * W - 1:2 * W], 1.0).then_inc(zeroed, 1)
            pool.wait_ge(zeroed, 8)

            def low_part(n):
                pool.wait_ge(hhi_ready, n * 2 + 2)
                pool.tensor_tensor(hlo[:, :], hT[:, :], hhi[:, :].bitcast(F32), ALU.subtract).then_inc(hlo_ready, 1)

            low_part(0)

            def sums_of_residuals(grp, i):
                pool.wait_ge(drained[grp.slot[("wo",)][0]], grp.drained(("wo",), i))
                pool.tensor_tensor(x01[:, :, :], xr[:, :, :], x1[:, :, :], ALU.add).then_inc(x01_ready, 1)

            with pool.Fori(0, ROUNDS) as i:
                sums_of_residuals(body, i)
                pool.wait_ge(x01_ready, i + 1)
                for s, half in KBD_ORDER:
                    if s == 0:
                        name = ("k", 4 * half + 3)
                        pool.wait_ge(drained[body.slot[name][0]], body.drained(name, i))
                    if s >= 2 and half == 0:
                        name = ("sc", (s - 1) * NQ - 1)
                        pool.wait_ge(filled[body.slot[name][0]], body.filled(name, i))
                    ms = slice(4 * half, 4 * half + 4)
                    for h in range(2):
                        r = slice(h * DH, (h + 1) * DH)
                        pool.tensor_tensor(KBD[r, s % 2, ms, h, :], KT[r, ms, s * P:(s + 1) * P],
                                           KBD[r, s % 2, ms, 1 - h, :], ALU.add).then_inc(kbd_ready, 1)
                pool.wait_ge(kbd_ready, i * (4 * NS) + 4 * NS)
                low_part(i + 1)
                pool.wait_ge(xo_ready, i + 1)
                pool.dma_start(t["x_mid"][bass.ds(i, 1), :, :].rearrange("a p n -> (a p) n"),
                               xo[:, :, :].rearrange("p s d -> p (s d)")).then_inc(xo_stored, 16)
                pool.wait_ge(xo_stored, i * 16 + 16)
                pool.sem_inc(xo_free, 1)
            sums_of_residuals(final, 0)
            pool.wait_ge(xo_ready, ROUNDS + 1)
            pool.dma_start(t["x_mid"][ROUNDS, :, :], xo[:, :, :].rearrange("p s d -> p (s d)")).then_inc(xo_stored, 16)
            pool.wait_ge(xo_stored, 16 * (ROUNDS + 1))

        @block.scalar
        def _(act):
            act.wait_ge(w_loaded, 64)
            act.activation(tmp[:, 0, :], w1raw, ACT.Abs, accum_out=wabs[:, 0:1]).then_inc(wabs_ready, 1)
            act.activation(tmp[:, 1, :], w2raw, ACT.Abs, accum_out=wabs[:, 1:2]).then_inc(wabs_ready, 1)
            act.wait_ge(zeroed, 8)
            act.wait_ge(w2_loaded, 16 * W2_DMAS)

            def run(steps, grp, i):
                def full(name):
                    act.wait_ge(filled[grp.slot[name][0]], grp.filled(name, i))
                    return bank[grp.slot[name][0]]

                def freed(name, ins):
                    ins.then_inc(drained[grp.slot[name][0]], 1)

                def affine(name, out, k):
                    return act.activation(out, full(name)[:, :], ACT.Identity, scale=lng[:, 2 * k:2 * k + 1], bias=lng[:, 2 * k + 1:2 * k + 2])

                for st in steps:
                    kind = st[0]
                    if kind == "x1T":
                        affine(st, hT[:, :], 0).then_inc(hhi_ready, 1)
                        freed(st, affine(st, hhi[:, :], 0))
                        act.wait_ge(drained[grp.slot[st][0]], grp.drained(st, i))
                        act.sem_inc(hhi_ready, 1)
                    elif kind in ("x2T", "x3T"):
                        freed(st, affine(st, hT2[:, :], 1 if kind == "x2T" else 2))
                    elif kind in "qk":
                        n = st[1] + NM * (kind == "k")
                        ps = full(st)
                        if n == 0:
                            full(("wo",))
                        if n == 3:
                            act.wait_ge(x01_ready, i + 1)
                            act.activation(xr[:, :, :], xs[:, :, :], ACT.Copy).then_inc(x_used, 1)
                        if n >= 4:
                            if n % 2 == 0:
                                act.wait_ge(phi_ready, i * NM + (n // 2 - 1))
                            else:
                                act.wait_ge(drained[grp.slot[blocks[n - 4]][0]], grp.drained(blocks[n - 4], i))
                        act.activation(tmp[:, n % 4, :], ps[:, :], ACT.Exp).then_inc(exp_ready, 1)
                        if n % 2 == 0:
                            dst = QT if kind == "q" else KT
                            freed(st, act.activation(dst[:, st[1], :], ps[:, :], ACT.Relu))
                    elif kind == "v":
                        _, s, h = st
                        ps = full(st)[:, :].rearrange("p (m h d) -> p m h d", h=2, d=DH)
                        act.activation(V[:, s % 2, 4 * h:4 * h + 4, 0, 0:DH], ps[:, :, 0, :], ACT.Copy)
                        freed(st, act.activation(V[:, s % 2, 4 * h:4 * h + 4, 1, W:W + DH], ps[:, :, 1, :], ACT.Copy))
                    elif kind == "kt":
                        _, s, h = st
                        freed(st, act.activation(Ktok[:, s % 2, 512 * h:512 * h + 512], full(st)[:, :], ACT.Copy))
                    elif kind == "tr":
                        s, half = st[1] // 2, st[1] % 2
                        freed(st, act.activation(QT[:, 4 * half:4 * half + 4, s * P:(s + 1) * P],
                                                 full(st)[:, :].rearrange("p (m q) -> p m q", q=P), ACT.Copy))
                    elif kind == "f1":
                        freed(st, act.activation(GT[:, st[1], :], full(st)[:, :], ACT.Gelu))
                    elif kind == "w1":
                        act.wait_ge(drained[grp.slot[st][0]], grp.drained(st, i))
                        act.activation(hb[:, st[1], :], hb[:, st[1], :], ACT.Gelu).then_inc(hact_ready, 1)
                    elif kind == "hT":
                        m = st[1]
                        freed(st, act.activation(GT[:, m, :], full(st)[:, :], ACT.Identity, scale=hln[:, 0, m:m + 1], bias=hln[:, 1, m:m + 1]))

            run([("x1T",)], first, 0)
            with act.Fori(0, ROUNDS) as i:
                run(steps, body, i)
            run([st for st in steps if st[0] in TAIL], final, 0)

        @block.vector
        def _(dve):
            count, base = [0], [0]

            def step(ins):
                count[0] += 1
                ins.then_inc(dve_step, 1)
                return count[0]

            def settle(n=None):
                dve.wait_ge(dve_step, base[0] + (count[0] if n is None else n))

            def do(ins):
                step(ins)
                settle()

            def stats(src, k):
                for s in range(NS):
                    n = step(dve.bn_stats(bst[:, k, s, :], src[:, s, :]))
                    yield
                settle(n)
                dve.memset(pad[:, :], 0.0)
                for s in range(NS):
                    n = step(dve.bn_aggr(mv[:, k, s, :], bst[:, k, s, :]))
                yield
                settle(n)

            def rstds(var, k, out):
                y, u, x = rs[:, k, out, :], rs[:, k, 1, :], rs[:, k, 3, :]
                n = step(dve.tensor_scalar(x, var, 1e-5, None, ALU.add))
                yield
                for ins in rsqrt_steps(dve, y, u, x):
                    settle(n)
                    n = step(ins())
                    yield
                settle(n)

            def normalise(src, dst, k, out, ready):
                for s in range(NS):
                    ins = dve.tensor_scalar(dst[:, s, :], src[:, s, :], mv[:, k, s, 0:1], rs[:, k, out, s:s + 1], ALU.subtract, ALU.mult)
                    if s < NS - 1 or ready is None:
                        step(ins)
                    else:
                        ins.then_inc(ready, 1)
                    yield

            def layernorm(src, dst, ready, k):
                yield from stats(src, k)
                yield from rstds(mv[:, k, :, 1], k, 0)
                yield from normalise(src, dst, k, 0, ready)

            dve.wait_ge(w_loaded, 64)
            for j, wraw in enumerate((w1raw, w2raw)):
                k = setup.slot[("wsum", j)][0]
                dve.wait_ge(filled[k], setup.filled(("wsum", j), 0))
                sc, inv = rs[:, 1, 2, 2 * j:2 * j + 1], rs[:, 1, 2, 2 * j + 1:2 * j + 2]
                do(dve.tensor_scalar(sc, bank[k][:, 0:1], 1.0 / (HF * D), 1e-5, ALU.mult, ALU.max))
                do(dve.reciprocal(sc, sc))
                do(dve.reciprocal(inv, sc))
                q = tmp[:, j, :]
                do(dve.tensor_scalar(q, wraw, sc, 2.0, ALU.mult, ALU.min))
                do(dve.tensor_scalar(q, q, -2.0, ROUND, ALU.max, ALU.add))
                do(dve.tensor_scalar(q, q, ROUND, 1.0, ALU.subtract, ALU.min))
                do(dve.tensor_scalar(q, q, -1.0, inv, ALU.max, ALU.mult))
                do(dve.tensor_tensor(q, q, wraw, ALU.subtract))
                dve.tensor_tensor(q, wraw, q, ALU.add).then_inc(wq_ready, 1)
                k = setup.slot[("wT", j)][0]
                dve.wait_ge(filled[k], setup.filled(("wT", j), 0))
                dst = w1T[:, :] if j == 0 else w2T[:, :, :].rearrange("p m d -> p (m d)")
                dve.tensor_copy(dst, bank[k][:, :]).then_inc(wT_ready, 1)
            dve.wait_ge(wT_ready, 2)
            dve.wait_ge(w2_loaded, 16 * W2_DMAS)
            do(dve.tensor_copy(whi[:, :, :], wqkv_raw))
            do(dve.tensor_tensor(wlo[:, :, :], wqkv_raw, whi[:, :, :].bitcast(F32), ALU.subtract))
            dve.memset(QT[:, :, :], 0.0).then_inc(split_w, 1)
            dve.wait_ge(split_w, 1)
            dve.wait_ge(zeroed, 8)
            setup_steps = count[0]

            def run(steps, grp, i, late):
                weaving = [iter(()), iter(())]
                turn = [0]

                def weave(n):
                    for _ in range(n):
                        turn[0] = 1 - turn[0]
                        if next(weaving[turn[0]], True):
                            next(weaving[1 - turn[0]], None)

                def finish(lane=0):
                    for _ in weaving[lane]:
                        pass

                def full(name):
                    dve.wait_ge(filled[grp.slot[name][0]], grp.filled(name, i))
                    return bank[grp.slot[name][0]]

                def written(name):
                    dve.wait_ge(drained[grp.slot[name][0]], grp.drained(name, i))

                def freed(name, ins):
                    ins.then_inc(drained[grp.slot[name][0]], 1)

                def after_wo():
                    yield from layernorm(x1, xn2, xn2_ready, 1)

                def after_f2():
                    yield from stats(x01, 1)
                    yield from rstds(mv[:, 1, :, 1], 1, 0)
                    r, r2, u = rs[:, 1, 0, :], rs[:, 1, 2, :], rs[:, 1, 1, :]
                    n = step(dve.tensor_tensor(u, r, r, ALU.mult))
                    yield
                    settle(n)
                    n = step(dve.tensor_tensor(u, u, mv[:, 1, :, 1], ALU.mult))
                    yield
                    settle(n)
                    yield from rstds(u, 1, 2)
                    n = step(dve.tensor_tensor(r2, r2, r, ALU.mult))
                    yield
                    settle(n)
                    yield from normalise(x01, xn2, 1, 2, xn2_ready)
                    yield from normalise(x01, xa, 1, 0, None)

                def after_w1():
                    dve.wait_ge(hact_ready, late * NS + NS)
                    yield from layernorm(hb, hb, hn_ready, 1)

                def after_w2():
                    settle()
                    n = step(dve.tensor_tensor(x1[:, :, :], xa[:, :, :], x1[:, :, :], ALU.add))
                    yield
                    settle(n)
                    dve.wait_ge(xo_free, late + PRIMED)
                    yield from layernorm(x1, xo, xo_ready, 1)

                def next_tile():
                    dve.wait_ge(x_loaded, i * 16 + 32)
                    yield from layernorm(xs, xn, xn_ready, 0)

                tokens = lambda ap: ap[:, :].rearrange("p (s d) -> p s d", d=D)
                for st in steps:
                    kind = st[0]
                    if kind == "wo":
                        ps = full(st)
                        dve.wait_ge(x_used, late + PRIMED)
                        freed(st, dve.tensor_tensor(x1[:, :, :], xr[:, :, :], tokens(ps), ALU.add))
                        written(st)
                        weaving[0] = after_wo()
                    elif kind in ("x2T", "x3T"):
                        finish()
                    elif kind == "x1T":
                        finish(1)
                    elif kind in "qk":
                        n = st[1] + NM * (kind == "k")
                        e, dst = tmp[:, n % 4, :], (QT if kind == "q" else KT)[:, st[1], :]
                        if n % 2 == 0:
                            written(st)
                            dve.scalar_tensor_tensor(dst, e, 1.0, dst, ALU.min, ALU.add).then_inc(phi_ready, 1)
                        else:
                            dve.wait_ge(exp_ready, i * (2 * NM) + (n + 1))
                            k = step(dve.tensor_scalar(e, e, 1.0, None, ALU.min))
                            weave(3)
                            settle(k)
                            freed(st, dve.scalar_tensor_tensor(dst, full(st)[:, :], 0.0, e, ALU.max, ALU.add))
                        weave(3)
                    elif kind == "sc":
                        n = st[1]
                        ps = full(st)
                        freed(st, dve.tensor_tensor(PT[:, n % 4, :, :], ps[:, :].rearrange("p (h q) -> p h q", q=P),
                                                    mask[:, :].unsqueeze(1).broadcast_to([P, 4, P]), ALU.mult))
                        weave(4)
                        if n == 2:
                            weaving[1] = next_tile()
                    elif kind == "av":
                        n = st[1]
                        s, q = n // NQ, n % NQ
                        ps = full(st)[:, 0:4 * W].rearrange("p (h w) -> p h w", w=W)
                        r = rden[:, n % 4, :]
                        k = step(dve.tensor_scalar(r, ps[:, :, DH], 1e-6, None, ALU.max))
                        weave(1)
                        settle(k)
                        k = step(dve.reciprocal(r, r))
                        weave(1)
                        settle(k)
                        freed(st, dve.tensor_tensor(AO[:, s % 2, q * 256:(q + 1) * 256].rearrange("p (h d) -> p h d", d=DH),
                                                    ps[:, :, 0:DH], r.unsqueeze(2).broadcast_to([P, 4, DH]), ALU.mult))
                        weave(3)
                    elif kind == "st":
                        _, s, r = st
                        a, b = PAIRS[r]
                        ps = full(st)[:, 0:(b - a) * 2 * W].rearrange("p (m w) -> p m w", w=2 * W)
                        for h in range(2):
                            rows, cols = slice(h * DH, (h + 1) * DH), slice(h * W, (h + 1) * W)
                            ins = dve.tensor_tensor(S[rows, s, a:b, cols], S[rows, s, a:b, cols], ps[rows, :, cols], ALU.add)
                        freed(st, ins)
                        weave(1)
                    elif kind == "f2":
                        ps = full(st)
                        dve.wait_ge(x01_ready, late + 1)
                        freed(st, dve.tensor_tensor(x01[:, :, :], x01[:, :, :], tokens(ps), ALU.add))
                        written(st)
                        weaving[0] = after_f2()
                    elif kind == "w1":
                        ps = full(st)
                        freed(st, dve.tensor_tensor(hb[:, st[1], :], ps[:, :], b1r[:, :], ALU.add))
                        if st[1] == NS - 1:
                            weaving[0] = after_w1()
                    elif kind == "hT" and st[1] == 0:
                        finish()
                    elif kind == "w2":
                        ps = full(st)
                        freed(st, dve.tensor_tensor(x1[:, :, :], tokens(ps), b2r[:, :].unsqueeze(1).broadcast_to([P, NS, D]), ALU.add))
                        written(st)
                        weaving[0] = after_w2()
                finish()
                dve.wait_ge(xo_ready, late + 1)
                if grp is body:
                    written(("st", NS - 1, len(PAIRS) - 1))

            RSTD = 1 + RSQRT_STEPS
            LN = 2 * NS + RSTD + NS - 1
            DVE_ROUND = 5 * LN + (RSTD + 3 + NS) + 1 + 2 * NS * NQ + NM
            base[0], count[0] = 0, setup_steps
            dve.wait_ge(x_loaded, 16)
            for _ in layernorm(xs, xn, xn_ready, 0):
                pass
            setup_steps = count[0]
            with dve.Fori(0, NG) as g:
                dve.memset(S[0:DH, :, :, 0:W], 0.0).then_inc(state_ready, 1)
                dve.memset(S[DH:P, :, :, W:2 * W], 0.0).then_inc(state_ready, 1)
                dve.wait_ge(state_ready, g * 2 + 2)
                dve.memset(pad[:, :], 0.0)
                with dve.Fori(0, NC) as c:
                    i = g * NC + c
                    base[0], count[0] = i * DVE_ROUND + setup_steps, 0
                    run(steps, body, i, i)
                    assert count[0] == DVE_ROUND, count[0]
            base[0], count[0] = ROUNDS * DVE_ROUND + setup_steps, 0
            run([st for st in steps if st[0] in TAIL], final, 0, ROUNDS)

        @block.tensor
        def _(pe):
            pe.wait_ge(zeroed, 8)
            pe.wait_ge(w_loaded, 64)
            pe.wait_ge(wabs_ready, 2)
            for j in range(2):
                k = setup.slot[("wsum", j)][0]
                pe.matmul(bank[k][:, 0:1], ones[:, :], wabs[:, j:j + 1], start=True, stop=True).then_inc(filled[k], 1)
            for j in range(2):
                pe.wait_ge(wq_ready, j + 1)
                k = setup.slot[("wT", j)][0]
                for m in range(NF):
                    ins = pe.transpose(bank[k][:, m * P:(m + 1) * P], tmp[:, j, m * P:(m + 1) * P], ident[:, :])
                ins.then_inc(filled[k], 1)
            pe.wait_ge(wT_ready, 2)
            pe.wait_ge(split_w, 1)

            def run(steps, grp, i, g, late, tile):
                def take(name):
                    k = grp.slot[name][0]
                    pe.wait_ge(drained[k], grp.free(name, i))
                    return bank[k]

                def fill(name, ins):
                    ins.then_inc(filled[grp.slot[name][0]], 1)

                def ready(name):
                    k = grp.slot[name][0]
                    pe.wait_ge(drained[k], grp.drained(name, i))

                def transposes(name, x):
                    ps = take(name)
                    for s in range(NS):
                        ins = pe.transpose(ps[:, s * P:(s + 1) * P], x[:, s, :], ident[:, :])
                    fill(name, ins)

                for st in steps:
                    kind = st[0]
                    if kind == "wo":
                        ps = take(st)
                        for s in range(NS):
                            for m in range(NM):
                                ins = pe.matmul(ps[:, s * P:(s + 1) * P], QT[:, m, s * P:(s + 1) * P], wo[:, m, :], start=(m == 0), stop=(m == NM - 1))
                        fill(st, ins)
                    elif kind == "x1T":
                        pe.wait_ge(xn_ready, tile + 1)
                        transposes(st, xn)
                    elif kind in "qk":
                        w, m = "qk".index(kind), slice(st[1] * P, (st[1] + 1) * P)
                        if st == ("q", 0):
                            pe.wait_ge(hlo_ready, i + 1)
                        ps = take(st)
                        pe.matmul(ps[:, :], whi[:, w, m], hhi[:, :], start=True, stop=False)
                        pe.matmul(ps[:, :], whi[:, w, m], hlo[:, :], start=False, stop=False)
                        fill(st, pe.matmul(ps[:, :], wlo[:, w, m], hhi[:, :], start=False, stop=True))
                    elif kind == "v":
                        _, s, h = st
                        ps = take(st)
                        tok, cols = slice(s * P, (s + 1) * P), slice(h * 512, (h + 1) * 512)
                        pe.matmul(ps[:, :], hhi[:, tok], whi[:, 2, cols], start=True, stop=False)
                        pe.matmul(ps[:, :], hhi[:, tok], wlo[:, 2, cols], start=False, stop=False)
                        fill(st, pe.matmul(ps[:, :], hlo[:, tok], whi[:, 2, cols], start=False, stop=True))
                    elif kind == "kt":
                        _, s, h = st
                        if s == 0 and h == 0:
                            ready(("k", NM - 1))
                        ps = take(st)
                        for m in range(4):
                            ins = pe.transpose(ps[:, m * P:(m + 1) * P], KT[:, 4 * h + m, s * P:(s + 1) * P], ident[:, :])
                        fill(st, ins)
                    elif kind == "kbd":
                        s = st[1]
                        pe.wait_ge(kbd_ready, i * (4 * NS) + 2 * (KBD_ORDER.index((s, 0)) + 1))
                        if s == 0:
                            pe.wait_ge(state_ready, g * 2 + 2)
                    elif kind == "sc":
                        n = st[1]
                        s, q = n // NQ, n % NQ
                        if q == NQ // 2:
                            pe.wait_ge(kbd_ready, i * (4 * NS) + 2 * (KBD_ORDER.index((s, 1)) + 1))
                        ps = take(st)
                        for h in range(4):
                            m = 2 * q + h // 2
                            ins = pe.matmul(ps[:, h * P:(h + 1) * P], KBD[:, s % 2, m, h % 2, :], QT[:, m, s * P:(s + 1) * P], start=True, stop=True)
                        fill(st, ins)
                    elif kind == "av":
                        n = st[1]
                        s, q = n // NQ, n % NQ
                        ready(("sc", n))
                        if q == 0:
                            ready(("v", s, 1))
                        ps = take(st)
                        for j in range(2):
                            m = 2 * q + j
                            out = ps[:, 2 * j * W:2 * (j + 1) * W]
                            pe.matmul(out, QT[:, m, s * P:(s + 1) * P], S[:, s, m, :], start=True, stop=False, skip_group_check=True)
                            for h in range(2):
                                ins = pe.matmul(out, PT[:, n % 4, 2 * j + h, :], V[:, s % 2, m, h, :], start=False, stop=(h == 1), skip_group_check=True)
                        fill(st, ins)
                    elif kind == "st":
                        _, s, r = st
                        a, b = PAIRS[r]
                        if r == 0:
                            ready(("kt", s, 1))
                        ps = take(st)
                        for m in range(a, b):
                            both = V[:, s % 2, m, :, :].rearrange("p h w -> p (h w)")
                            both = both[:, 0:4 * W].rearrange("p (k w) -> p k w", w=W)[:, 0:4:3, :]
                            ins = pe.matmul(ps[:, (m - a) * 2 * W:(m - a + 1) * 2 * W], Ktok[:, s % 2, m * P:(m + 1) * P], both, start=True, stop=True)
                        fill(st, ins)
                    elif kind == "tr":
                        s, half = st[1] // 2, st[1] % 2
                        ready(("av", 4 * s + 2 * half + 1))
                        ps = take(st)
                        for m in range(4):
                            ins = pe.transpose(ps[:, m * P:(m + 1) * P], AO[:, s % 2, (4 * half + m) * P:(4 * half + m + 1) * P], ident[:, :])
                        fill(st, ins)
                    elif kind in ("x2T", "x3T"):
                        pe.wait_ge(xn2_ready, late * 2 + (1 if kind == "x2T" else 2))
                        transposes(st, xn2)
                        ready(st)
                    elif kind == "f1":
                        m = st[1]
                        ps = take(st)
                        fill(st, pe.matmul(ps[:, :], wf1[:, m * P:(m + 1) * P], hT2[:, :], start=True, stop=True))
                    elif kind in ("f2", "w2"):
                        ready(("f1" if kind == "f2" else "hT", NF - 1))
                        w = wf2 if kind == "f2" else w2T
                        ps = take(st)
                        for s in range(NS):
                            for m in range(NF):
                                ins = pe.matmul(ps[:, s * P:(s + 1) * P], GT[:, m, s * P:(s + 1) * P], w[:, m, :], start=(m == 0), stop=(m == NF - 1))
                        fill(st, ins)
                    elif kind == "w1":
                        s = st[1]
                        ps = take(st)
                        fill(st, pe.matmul(ps[:, :], hT2[:, s * P:(s + 1) * P], w1T[:, :], start=True, stop=True))
                    elif kind == "hT":
                        m = st[1]
                        if m == 0:
                            pe.wait_ge(hn_ready, late + 1)
                        ps = take(st)
                        for s in range(NS):
                            ins = pe.transpose(ps[:, s * P:(s + 1) * P], hb[:, s, m * P:(m + 1) * P], ident[:, :])
                        fill(st, ins)
                if grp is body:
                    ready(("tr", 2 * NS - 1))

            run([("x1T",)], first, 0, None, None, 0)
            with pe.Fori(0, NG) as g:
                with pe.Fori(0, NC) as c:
                    i = g * NC + c
                    run(steps, body, i, g, i, i + 1)
            run([st for st in steps if st[0] in TAIL], final, 0, None, ROUNDS, None)
    return final.after(1), setup.after(1)


def phase_b(nc, t, ctx, bank, filled, drained, last, ident):
    NB, T, D = t["L0_attn_x"].shape
    NC = T // P
    NH, KV, HD = 4, 2, 32
    SIDE = t["x_mid"].shape[2] // D
    NT, NL, LW = 3, 16, 64
    NM = NL * LW // P
    HC = NC // 2
    TREES = "qkv"

    units = [(j, h) for j in range(NC) for h in range(NH)]
    NU = len(units)

    def pieces(j):
        return [(a, min(4, j + 1 - a)) for a in range(0, j + 1, 4)]

    attn1 = []
    for u in range(NU + 6):
        if u < NU:
            attn1 += [("s", u, a) for a, _ in pieces(units[u][0])]
        if 0 <= u - 2 < NU:
            attn1 += [("t", u - 2, a) for a, _ in pieces(units[u - 2][0])]
        if 0 <= u - 3 < NU:
            attn1.append(("av", u - 3))
        if 0 <= u - 5 < NU and units[u - 5][1] == NH - 1:
            attn1.append(("at", units[u - 5][0]))
    fff = []
    for n in range(NT * NM + 2):
        if n < NT * NM:
            fff.append(("h", n))
        if n >= 2:
            fff.append(("o", n - 2))
    attn2 = []
    for j in range(NC + 2):
        if j < NC:
            attn2 += [("S", j, a) for a in range(2)]
        if 0 <= j - 1 < NC:
            attn2 += [("T", j - 1, a) for a in range(2)]
        if 0 <= j - 2 < NC:
            attn2.append(("A", j - 2))

    order = [("xT", a) for a in range(2)] + [("qkv", r) for r in range(NC // 2)]
    order += [("qt", c) for c in range(NC)] + [("kt", r) for r in range(NC // 2)]
    for st in attn1:
        if st[0] == "av":
            j, h = units[st[1]]
            if h == 0:
                order.append(("av", j))
        else:
            order.append(st)
    order += [("wo", a) for a in range(2)]
    for f in range(2):
        order += [("yT", f), ("nd", f), ("sl", f)]
        for st in fff:
            if st[0] == "h":
                order.append(("h", f, st[1]))
            elif st[1] % NM == 0:
                order.append(("o", f, st[1] // NM))
        order.append(("vt", f))
    order += attn2
    before, undrained = last
    pre = Groups([("pre", 0), ("pre", 1)], before, undrained)
    gb = Groups(order, pre.after(1), [a + b for a, b in zip(undrained, pre.per)], held=("av", "o"), held_banks=(6, 7))
    tgroups = [st for st in attn1 if st[0] == "t"]
    tindex = {st: n for n, st in enumerate(tgroups)}
    NTG = len(tgroups)
    SOFT = 1.0 / np.sqrt(np.float32(D))

    with ExitStack() as stack:
        sb = lambda name, shape, dt=F32: stack.enter_context(nc.sbuf_tensor("b_" + name, shape, dt))
        sem = lambda name: ctx.enter_context(nc.semaphore("b_" + name))

        wqkv = sb("wqkv", [P, 2 * D])
        wo = sb("wo", [P, D])
        normw = sb("normw", [P, 1])
        scal = sb("scal", [P, 4])
        W1 = sb("W1", [P, NT, NL * LW])
        W2 = sb("W2", [P, NT, NM, D])
        b1raw = sb("b1raw", [NT * NM, P])
        b1 = sb("b1", [P, NT * NM])
        nwraw = sb("nwraw", [96, D])
        nwT = sb("nwT", [P, 96])
        nthr = sb("nthr", [96, 2])
        b2 = sb("b2", [P, NT, D])
        maskw = sb("maskw", [96, NT * NM, P], BF16)
        path = sb("path", [96, P], BF16)
        identb = sb("identb", [P, P], BF16)
        causal = sb("causal", [P, P], BF16)

        X = sb("X", [P, NC, D])
        Y = sb("Y", [P, NC, D])
        O = sb("O", [P, NC, D])
        xn = sb("xn", [P, NC, D])
        hT = sb("hT", [P, T])
        sq = sb("sq", [P, NC, 6 * HD])
        QN = sb("QN", [P, NC, 6, HD])
        QS = sb("QS", [P, NC, NH, 4, HD])
        KS = sb("KS", [P, NC, KV, 4, HD])
        QST = sb("QST", [P, NC, NH, P], F32R)
        KST = sb("KST", [P, KV, T], F32R)
        V = sb("V", [P, NC, 96])
        Pb = sb("Pb", [P, 3, T])
        PTb = sb("PTb", [P, 4, 4, P])
        AO = sb("AO", [P, 2, D])
        AOT = sb("AOT", [P, T])
        mx = sb("mx", [P, 4, 2])
        nb = sb("nb", [P, 4])
        sums = sb("sums", [P, 2, NH, 2])
        rsum = sb("rsum", [P, 2, NH])
        yT = sb("yT", [P, 4 * P])
        Dm = sb("Dm", [96, 4 * P], BF16)
        sel = sb("sel", [P, 4 * P])
        Hb = sb("Hb", [P, 4, 4 * P])
        F = sb("F", [P, 2, T])
        FvT = sb("FvT", [P, 4 * P])
        Fv = sb("Fv", [P, NC, D])
        pad = sb("pad", [P, 1])
        prime = sb("prime", [P, NBANK + 2])
        bst = sb("bst", [P, NC, 6])
        mv = sb("mv", [P, NC, 2])
        rs = sb("rs", [P, 4, 48])

        w_loaded, zeroed, pre_ready = sem("w_loaded"), sem("zeroed"), sem("pre_ready")
        x_loaded, x_used = sem("x_loaded"), sem("x_used")
        xn_ready, sq_ready = sem("xn_ready"), sem("sq_ready")
        split_ready = sem("split_ready")
        nb_ready, p_ready, av_done = sem("nb_ready"), sem("p_ready"), sem("av_done")
        y_ready, out_ready = sem("y_ready"), sem("out_ready")
        out_stored, out_free = sem("out_stored"), sem("out_free")
        nb2_ready, p2_ready, av2_done = sem("nb2_ready"), sem("p2_ready"), sem("av2_done")
        h_used = sem("h_used")
        dve_step, act_step = sem("dve_step"), sem("act_step")

        block = stack.enter_context(nc.Block())
        column = lambda ap: ap.rearrange("(p a) -> p a", a=1)
        wide_maskw = Pb[0:96, :, :].rearrange("p a n -> p (a n)").rearrange("p (n c) -> p n c", c=P)
        wide_path, wide_causal = xn[0:96, 0, :], xn[:, 1, :]
        loads = [(wqkv[:, 0:D], t["L1_attn_Wq"]), (wqkv[:, D:D + 64], t["L1_attn_Wk"]), (wqkv[:, D + 64:], t["L1_attn_Wv"]),
                 (wo[:, :], t["L1_attn_Wo"]), (normw[:, :], column(t["L1_attn_norm_w"])),
                 (scal[:, 0:1], t["L1_attn_gate"].rearrange("(p a) -> p a", a=1).broadcast_to([P, 1])),
                 (scal[:, 1:2], t["L1_attn_log_temperature"].rearrange("(p a) -> p a", a=1).broadcast_to([P, 1])),
                 (wide_maskw, t["c_maskw"]), (wide_path, t["c_path"]), (wide_causal, t["c_causal"]),
                 (nthr[:, 1:2], t["c_comp"])]
        for n, k in enumerate(TREES):
            loads += [(W1[:, n, :].rearrange("p (l h) -> p l h", l=NL), t[f"L1_ffn_{k}_w1"].rearrange("l d h -> d l h")),
                      (W2[:, n, :, :], t[f"L1_ffn_{k}_w2"].rearrange("(m a) h d -> (a h) m d", a=2)),
                      (b1raw[n * NM:(n + 1) * NM, :], t[f"L1_ffn_{k}_b1"].rearrange("(m a) h -> m (a h)", a=2))]
            for a in range(2):
                r = 32 * n + (NL - 1) * a
                loads += [(nwraw[r:r + NL - 1, :], t[f"L1_ffn_{k}_node_w"]), (nthr[r:r + NL - 1, 0:1], column(t[f"L1_ffn_{k}_node_b"]))]
            loads.append((b2[32 * n:32 * n + NL, n, :], t[f"L1_ffn_{k}_b2"]))

        @block.sync
        def _(sp):
            sp.wait_ge(zeroed, 5)
            for dst, src in loads:
                sp.dma_start(dst, src).then_inc(w_loaded, 16)
            with sp.Fori(0, NB // SIDE) as g:
                with sp.Fori(0, SIDE) as s:
                    sp.wait_ge(x_used, g * (2 * SIDE) + s * 2 + PRIMED)
                    sp.dma_start(X[:, :, :], t["x_mid"][bass.ds(g * NC + 1, NC), :, bass.ds(s * D, D)]
                                 .rearrange("c p d -> p c d")).then_inc(x_loaded, 16)

        @block.gpsimd
        def _(pool):
            for n, primed in enumerate((x_used, out_free)):
                pool.memset(prime[:, n:n + 1], 0.0).then_inc(primed, PRIMED)
            pool.memset(nwraw[:, :], 0.0).then_inc(zeroed, 1)
            pool.memset(nthr[:, :], 0.0).then_inc(zeroed, 1)
            pool.memset(b2[:, :, :], 0.0).then_inc(zeroed, 1)
            pool.memset(b1raw[:, :], 0.0).then_inc(zeroed, 1)
            pool.memset(V[:, :, 64:96], 0.0).then_inc(zeroed, 1)
            with pool.Fori(0, NB) as b:
                for a in range(2):
                    pool.wait_ge(out_ready, b * 2 + (a + 1))
                    pool.dma_start(t["out"].rearrange("b (c p) d -> b p c d", p=P)[bass.ds(b, 1), :, a * HC:(a + 1) * HC, :]
                                   .rearrange("b p c d -> p (b c) d"), O[:, a * HC:(a + 1) * HC, :]).then_inc(out_stored, 16)
                pool.wait_ge(out_stored, b * 32 + 32)
                pool.sem_inc(out_free, 1)

        def full(eng, name, b):
            k = gb.slot[name][0]
            eng.wait_ge(filled[k], gb.filled(name, b))
            return bank[k]

        def freed(name, ins):
            ins.then_inc(drained[gb.slot[name][0]], 1)

        def evacuated(eng, name, b):
            eng.wait_ge(drained[gb.slot[name][0]], gb.drained(name, b))

        @block.scalar
        def _(act):
            act.wait_ge(w_loaded, 16 * len(loads))
            act.activation(scal[:, 2:3], scal[:, 1:2], ACT.Exp).then_inc(act_step, 1)
            act.wait_ge(act_step, 1)
            act.activation(scal[:, 3:4], scal[:, 2:3], ACT.Copy, scale=-1.0).then_inc(pre_ready, 1)
            with act.Fori(0, NB) as b:
                for a in range(2):
                    ps = full(act, ("xT", a), b)
                    freed(("xT", a), act.activation(hT[:, a * 512:(a + 1) * 512], ps[:, :], ACT.Copy, scale=normw[:, 0:1]))
                for r in range(NC // 2):
                    ps = full(act, ("qkv", r), b)[:, :].rearrange("p (c n) -> p c n", c=2)
                    act.activation(sq[:, 2 * r:2 * r + 2, :], ps[:, :, 0:192], ACT.Square)
                    act.activation(V[:, 2 * r:2 * r + 2, 0:64], ps[:, :, 192:256], ACT.Copy).then_inc(sq_ready, 1)
                for c in range(NC):
                    ps = full(act, ("qt", c), b)
                    freed(("qt", c), act.activation(QST[:, c, :, :].rearrange("p h q -> p (h q)"), ps[:, :], ACT.Copy))
                for r in range(NC // 2):
                    ps = full(act, ("kt", r), b)[:, :].rearrange("p (c v k) -> p v c k", c=2, v=KV)
                    freed(("kt", r), act.activation(KST[:, :, r * 256:(r + 1) * 256].rearrange("p v (c k) -> p v c k", c=2), ps, ACT.Copy))
                for u, (j, h) in enumerate(units):
                    act.wait_ge(nb_ready, b * NU + (u + 1))
                    if u >= 3:
                        act.wait_ge(filled[gb.slot[("t", u - 3, pieces(units[u - 3][0])[-1][0])][0]],
                                    gb.filled(("t", u - 3, pieces(units[u - 3][0])[-1][0]), b))
                    for r, (a, n) in enumerate(pieces(j)):
                        ps = full(act, ("s", u, a), b)
                        act.activation(Pb[:, u % 3, a * P:(a + n) * P], ps[:, 0:n * P], ACT.Exp, scale=scal[:, 2:3], bias=nb[:, u % 4:u % 4 + 1],
                                       accum_out=sums[:, j % 2, h, r:r + 1]).then_inc(drained[gb.slot[("s", u, a)][0]], 1)
                for f in range(2):
                    ps = full(act, ("yT", f), b)
                    freed(("yT", f), act.activation(yT[:, :], ps[:, :], ACT.Copy))
                    ps = full(act, ("sl", f), b)
                    freed(("sl", f), act.activation(sel[:, :], ps[:, :], ACT.Relu, bias=1.0))
                    for st in fff:
                        n = st[1]
                        if st[0] == "h":
                            if n >= 4:
                                act.wait_ge(h_used, (b * 2 + f) * (NT * NM) + (n - 3))
                            ps = full(act, ("h", f, n), b)
                            freed(("h", f, n), act.activation(Hb[:, n % 4, :], ps[:, :], ACT.Relu, bias=b1[:, n:n + 1]))
                    ps = full(act, ("vt", f), b)
                    freed(("vt", f), act.activation(Fv[:, f * HC:(f + 1) * HC, :].rearrange("p c d -> p (c d)"), ps[:, :], ACT.Copy))
                for j in range(NC):
                    act.wait_ge(nb2_ready, b * NC + (j + 1))
                    if j >= 3:
                        act.wait_ge(filled[gb.slot[("T", j - 3, 1)][0]], gb.filled(("T", j - 3, 1), b))
                    for a in range(2):
                        ps = full(act, ("S", j, a), b)
                        act.activation(Pb[:, j % 3, a * 512:(a + 1) * 512], ps[:, :], ACT.Exp, scale=float(SOFT), bias=nb[:, j % 4:j % 4 + 1],
                                       accum_out=sums[:, j // 4, j % 4, a:a + 1]).then_inc(drained[gb.slot[("S", j, a)][0]], 1)

        @block.vector
        def _(dve):
            count, base = [0], [0]

            def step(ins):
                count[0] += 1
                ins.then_inc(dve_step, 1)

            def settle():
                dve.wait_ge(dve_step, base[0] + count[0])

            def do(ins):
                step(ins)
                settle()

            def rsqrt(x, n):
                y, u = rs[:, 0, 0:n], rs[:, 1, 0:n]
                do(dve.tensor_scalar(u.bitcast(I32), x.bitcast(I32), 1, None, ALU.logical_shift_right))
                do(dve.tensor_scalar(y.bitcast(I32), u.bitcast(I32), -1.0, float(0x5F3759DF), ALU.mult, ALU.add))
                for _ in range(3):
                    do(dve.tensor_tensor(u, y, y, ALU.mult))
                    do(dve.scalar_tensor_tensor(u, u, -0.5, x, ALU.mult, ALU.mult))
                    do(dve.scalar_tensor_tensor(y, u, 1.5, y, ALU.add, ALU.mult))
                return y

            def stats(src, cs):
                for c in cs:
                    step(dve.bn_stats(bst[:, c, :], src[:, c, :]))
                settle()
                dve.memset(pad[:, :], 0.0)
                for c in cs:
                    step(dve.bn_aggr(mv[:, c, :], bst[:, c, :]))
                settle()

            def layernorm(src, dst, cs, ready):
                cs = list(cs)
                stats(src, cs)
                do(dve.tensor_scalar(rs[:, 3, 0:len(cs)], mv[:, cs[0]:cs[-1] + 1, 1], 1e-5, None, ALU.add))
                y = rsqrt(rs[:, 3, 0:len(cs)], len(cs))
                for n, c in enumerate(cs):
                    ins = dve.tensor_scalar(dst[:, c, :], src[:, c, :], mv[:, c, 0:1], y[:, n:n + 1], ALU.subtract, ALU.mult)
                    if n < len(cs) - 1:
                        step(ins)
                    else:
                        ins.then_inc(ready, 1)

            dve.wait_ge(w_loaded, 16 * len(loads))
            dve.tensor_scalar(nthr[:, 0:1], nthr[:, 0:1], -1.0, None, ALU.mult).then_inc(dve_step, 1)
            for dst, src in ((maskw[:, :, :], wide_maskw), (path[:, :], wide_path), (causal[:, :], wide_causal), (identb[:, :], ident[:, :])):
                dve.tensor_copy(dst, src).then_inc(pre_ready, 1)
            for n, (dst, rows) in enumerate(((nwT[:, :], 96), (b1[:, :], NT * NM))):
                k = pre.slot[("pre", n)][0]
                dve.wait_ge(filled[k], pre.filled(("pre", n), 0))
                dve.tensor_copy(dst, bank[k][:, 0:rows]).then_inc(pre_ready, 1)
            dve.wait_ge(pre_ready, 7)
            dve.wait_ge(zeroed, 5)
            dve.wait_ge(dve_step, 1)
            PER = 299

            with dve.Fori(0, NB) as b:
                base[0], count[0] = b * PER + 1, 0
                dve.wait_ge(x_loaded, b * 16 + 16)
                stats(X, range(NC))
                do(dve.tensor_tensor(rs[:, 2, 0:NC], mv[:, :, 0], mv[:, :, 0], ALU.mult))
                do(dve.scalar_tensor_tensor(rs[:, 3, 0:NC], rs[:, 2, 0:NC], 1e-6, mv[:, :, 1], ALU.add, ALU.add))
                y = rsqrt(rs[:, 3, 0:NC], NC)
                for c in range(NC):
                    ins = dve.tensor_scalar(xn[:, c, :], X[:, c, :], y[:, c:c + 1], None, ALU.mult)
                    if c % HC == HC - 1:
                        ins.then_inc(xn_ready, 1)
                    else:
                        step(ins)
                for r in range(NC // 2):
                    dve.wait_ge(sq_ready, b * (NC // 2) + (r + 1))
                    step(dve.tensor_reduce(rs[:, 3, 12 * r:12 * r + 12], sq[:, 2 * r:2 * r + 2, :].rearrange("p c (h d) -> p (c h) d", d=HD), AX.X, ALU.add))
                settle()
                do(dve.tensor_scalar(rs[:, 3, 0:48], rs[:, 3, 0:48], 1e-24, None, ALU.max))
                y = rsqrt(rs[:, 3, 0:48], 48)
                for r in range(NC // 2):
                    ps = full(dve, ("qkv", r), b)[:, :].rearrange("p (c n) -> p c n", c=2)[:, :, 0:192].rearrange("p c (h d) -> p c h d", d=HD)
                    freed(("qkv", r), dve.tensor_tensor(QN[:, 2 * r:2 * r + 2, :, :], ps,
                          y[:, 12 * r:12 * r + 12].rearrange("p (c h) -> p c h", c=2).unsqueeze(3).broadcast_to([P, 2, 6, HD]), ALU.mult))
                for r in range(NC // 2):
                    evacuated(dve, ("qkv", r), b)
                for c in range(NC):
                    for src, dst, his, los in ((QN[:, c, 0:NH, :], QS, (0, 1), (2, 3)), (QN[:, c, NH:, :], KS, (0, 2), (1, 3))):
                        for n in his:
                            step(dve.tensor_copy(dst[:, c, :, n, :].bitcast(F32R), src))
                settle()
                for c in range(NC):
                    for src, dst, his, los in ((QN[:, c, 0:NH, :], QS, (0, 1), (2, 3)), (QN[:, c, NH:, :], KS, (0, 2), (1, 3))):
                        for n in los:
                            ins = dve.tensor_tensor(dst[:, c, :, n, :].bitcast(F32R), src, dst[:, c, :, his[0], :], ALU.subtract)
                            if dst is KS and n == 3:
                                ins.then_inc(split_ready, 1)
                            else:
                                step(ins)
                for st in attn1:
                    if st[0] == "s":
                        u, a = st[1], st[2]
                        j, h = units[u]
                        ps = full(dve, st, b)
                        n = dict(pieces(j))[a]
                        if u >= 4 and a == 0:
                            dve.wait_ge(drained[gb.slot[("s", u - 4, pieces(units[u - 4][0])[-1][0])][0]],
                                        gb.drained(("s", u - 4, pieces(units[u - 4][0])[-1][0]), b))
                        do(dve.tensor_reduce(mx[:, u % 4, a // 4:a // 4 + 1], ps[:, 0:n * P], AX.X, ALU.max))
                        if a == pieces(j)[-1][0]:
                            if a:
                                dve.tensor_scalar(nb[:, u % 4:u % 4 + 1], mx[:, u % 4, 0:1], mx[:, u % 4, 1:2], scal[:, 3:4], ALU.max, ALU.mult)\
                                   .then_inc(nb_ready, 1)
                            else:
                                dve.tensor_scalar(nb[:, u % 4:u % 4 + 1], mx[:, u % 4, 0:1], scal[:, 3:4], None, ALU.mult).then_inc(nb_ready, 1)
                    elif st[0] == "t":
                        n = tindex[st]
                        if n >= 4:
                            dve.wait_ge(av_done, b * NU + (tgroups[n - 4][1] + 1))
                        ps = full(dve, st, b)
                        w = dict(pieces(units[st[1]][0]))[st[2]]
                        freed(st, dve.tensor_copy(PTb[:, n % 4, 0:w, :].rearrange("p k q -> p (k q)"), ps[:, 0:w * P]))
                    elif st[0] == "av" and units[st[1]][1] == NH - 1:
                        j = units[st[1]][0]
                        u = st[1]
                        last = ("s", u, pieces(j)[-1][0])
                        dve.wait_ge(drained[gb.slot[last][0]], gb.drained(last, b))
                        r = rsum[:, j % 2, :]
                        if len(pieces(j)) == 2:
                            do(dve.tensor_tensor(r, sums[:, j % 2, :, 0], sums[:, j % 2, :, 1], ALU.add))
                            do(dve.reciprocal(r, r))
                        else:
                            do(dve.reciprocal(r, sums[:, j % 2, :, 0]))
                        ps = full(dve, ("av", j), b)[:, 0:NH * 96].rearrange("p (h w) -> p h w", w=96)
                        for v in range(KV):
                            ins = dve.tensor_tensor(AO[:, j % 2, 64 * v:64 * v + 64].rearrange("p (h d) -> p h d", d=HD),
                                                    ps[:, 2 * v:2 * v + 2, HD * v:HD * v + HD],
                                                    r[:, 2 * v:2 * v + 2].unsqueeze(2).broadcast_to([P, 2, HD]), ALU.mult)
                        freed(("av", j), ins)
                    elif st[0] == "at":
                        j = st[1]
                        ps = full(dve, st, b)
                        freed(st, dve.tensor_copy(AOT[:, j * P:(j + 1) * P], ps[:, 0:P]))
                for a in range(2):
                    ps = full(dve, ("wo", a), b)[:, :].rearrange("p (c d) -> p c d", d=D)
                    cs = slice(a * HC, (a + 1) * HC)
                    freed(("wo", a), dve.scalar_tensor_tensor(Y[:, cs, :], ps, scal[:, 0:1], X[:, cs, :], ALU.mult, ALU.add))
                    evacuated(dve, ("wo", a), b)
                    dve.tensor_tensor(Y[:, cs, :], Y[:, cs, :], X[:, cs, :], ALU.add).then_inc(x_used, 1)
                    dve.wait_ge(x_used, b * 2 + (a + 1 + PRIMED))
                    layernorm(Y, Y, range(a * HC, (a + 1) * HC), y_ready)
                for f in range(2):
                    ps = full(dve, ("nd", f), b)
                    freed(("nd", f), dve.tensor_scalar(Dm[:, :], ps[0:96, :], nthr[:, 0:1], nthr[:, 1:2], ALU.is_ge, ALU.subtract))
                    for k in range(NT):
                        ps = full(dve, ("o", f, k), b)
                        dst = F[:, k, f * 512:(f + 1) * 512] if k < 2 else FvT[:, :]
                        freed(("o", f, k), dve.tensor_copy(dst, ps[:, :]))
                dve.wait_ge(out_free, b + PRIMED)
                for st in attn2:
                    j = st[1]
                    if st[0] == "S":
                        a = st[2]
                        ps = full(dve, st, b)
                        if a == 0 and j >= 4:
                            evacuated(dve, ("S", j - 4, 1), b)
                        do(dve.tensor_reduce(mx[:, j % 4, a:a + 1], ps[:, :], AX.X, ALU.max))
                        if a:
                            do(dve.tensor_scalar(mx[:, j % 4, 0:1], mx[:, j % 4, 0:1], mx[:, j % 4, 1:2], None, ALU.max))
                            dve.tensor_scalar(nb[:, j % 4:j % 4 + 1], mx[:, j % 4, 0:1], -float(SOFT), None, ALU.mult).then_inc(nb2_ready, 1)
                    elif st[0] == "T":
                        a = st[2]
                        if j >= 2:
                            dve.wait_ge(av2_done, b * NC + (j - 1))
                        ps = full(dve, st, b)
                        freed(st, dve.tensor_copy(PTb[:, (2 * j + a) % 4, :, :].rearrange("p k q -> p (k q)"), ps[:, :]))
                    else:
                        evacuated(dve, ("S", j, 1), b)
                        r = rsum[:, j % 2, 0:1]
                        do(dve.tensor_tensor(r, sums[:, j // 4, j % 4, 0:1], sums[:, j // 4, j % 4, 1:2], ALU.add))
                        do(dve.reciprocal(r, r))
                        ps = full(dve, st, b)
                        freed(st, dve.scalar_tensor_tensor(O[:, j, :], ps[:, 0:D], r, Y[:, j, :], ALU.mult, ALU.add))
                        evacuated(dve, st, b)
                        if j % HC == HC - 1:
                            layernorm(O, O, range(j - HC + 1, j + 1), out_ready)
                assert count[0] == PER, (count[0], PER)

        @block.tensor
        def _(pe):
            pe.wait_ge(w_loaded, 16 * len(loads))
            for n, (src, rows) in enumerate(((nwraw, 96), (b1raw, NT * NM))):
                k = pre.slot[("pre", n)][0]
                pe.transpose(bank[k][:, 0:rows], src[:, :], ident[0:rows, 0:rows]).then_inc(filled[k], 1)
            pe.wait_ge(pre_ready, 7)
            pe.wait_ge(zeroed, 5)
            with pe.Fori(0, NB) as b:

                def take(name):
                    k = gb.slot[name][0]
                    pe.wait_ge(drained[k], gb.free(name, b))
                    return bank[k]

                def fill(name, ins):
                    ins.then_inc(filled[gb.slot[name][0]], 1)

                def ready(name):
                    evacuated(pe, name, b)

                for a in range(2):
                    pe.wait_ge(xn_ready, b * 2 + (a + 1))
                    ps = take(("xT", a))
                    for c in range(HC):
                        ins = pe.transpose(ps[:, c * P:(c + 1) * P], xn[:, a * HC + c, :], ident[:, :])
                    fill(("xT", a), ins)
                for r in range(NC // 2):
                    ready(("xT", r // 2))
                    ps = take(("qkv", r))
                    for c in range(2):
                        ins = pe.matmul(ps[:, c * 256:(c + 1) * 256], hT[:, (2 * r + c) * P:(2 * r + c + 1) * P], wqkv[:, :], start=True, stop=True)
                    fill(("qkv", r), ins)
                for c in range(NC):
                    pe.wait_ge(split_ready, b * NC + (c + 1))
                    ps = take(("qt", c))
                    for h in range(NH):
                        ins = pe.transpose(ps[:, h * P:(h + 1) * P], QS[:, c, h, :, :].rearrange("p a d -> p (a d)"), ident[:, :])
                    fill(("qt", c), ins)
                for r in range(NC // 2):
                    ps = take(("kt", r))
                    for c in range(2):
                        for v in range(KV):
                            ins = pe.transpose(ps[:, (2 * c + v) * P:(2 * c + v + 1) * P], KS[:, 2 * r + c, v, :, :].rearrange("p a d -> p (a d)"), ident[:, :])
                    fill(("kt", r), ins)
                for c in range(NC):
                    ready(("qt", c))
                for r in range(NC // 2):
                    ready(("kt", r))
                for st in attn1:
                    if st[0] == "s":
                        u, a = st[1], st[2]
                        j, h = units[u]
                        n = dict(pieces(j))[a]
                        ps = take(st)
                        diag = a + n - 1 == j
                        ins = pe.matmul(ps[:, 0:n * P], QST[:, j, h, :], KST[:, h // 2, a * P:(a + n) * P], start=True, stop=not diag, skip_group_check=True)
                        if diag:
                            ins = pe.matmul(ps[:, (n - 1) * P:n * P], identb[:, :], causal[:, :], start=False, stop=True, skip_group_check=True)
                        fill(st, ins)
                    elif st[0] == "t":
                        u, a = st[1], st[2]
                        ready(("s", u, a))
                        ps = take(st)
                        for k in range(dict(pieces(units[u][0]))[a]):
                            ins = pe.transpose(ps[:, k * P:(k + 1) * P], Pb[:, u % 3, (a + k) * P:(a + k + 1) * P], ident[:, :])
                        fill(st, ins)
                    elif st[0] == "av":
                        u = st[1]
                        j, h = units[u]
                        ps = take(("av", j)) if h == 0 else bank[gb.slot[("av", j)][0]]
                        for a, n in pieces(j):
                            ready(("t", u, a))
                            for k in range(n):
                                ins = pe.matmul(ps[:, h * 96:(h + 1) * 96], PTb[:, tindex[("t", u, a)] % 4, k, :], V[:, a + k, :],
                                                start=(a + k == 0), stop=(a + k == j), skip_group_check=True)
                        ins.then_inc(av_done, 1)
                        if h == NH - 1:
                            pe.wait_ge(av_done, b * NU + (u + 1))
                            pe.nop().then_inc(filled[gb.slot[("av", j)][0]], 1)
                    else:
                        j = st[1]
                        ready(("av", j))
                        ps = take(st)
                        fill(st, pe.transpose(ps[:, 0:P], AO[:, j % 2, :], ident[:, :]))
                for a in range(2):
                    for j in range(a * HC, (a + 1) * HC):
                        ready(("at", j))
                    ps = take(("wo", a))
                    for c in range(HC):
                        ins = pe.matmul(ps[:, c * P:(c + 1) * P], AOT[:, (a * HC + c) * P:(a * HC + c + 1) * P], wo[:, :], start=True, stop=True)
                    fill(("wo", a), ins)
                for f in range(2):
                    pe.wait_ge(y_ready, b * 2 + (f + 1))
                    ps = take(("yT", f))
                    for c in range(HC):
                        ins = pe.transpose(ps[:, c * P:(c + 1) * P], Y[:, f * HC + c, :], ident[:, :])
                    fill(("yT", f), ins)
                    ready(("yT", f))
                    ps = take(("nd", f))
                    fill(("nd", f), pe.matmul(ps[0:96, :], nwT[:, :], yT[:, :], start=True, stop=True))
                    ready(("nd", f))
                    ps = take(("sl", f))
                    fill(("sl", f), pe.matmul(ps[:, :], path[:, :], Dm[:, :], start=True, stop=True))
                    for st in fff:
                        n = st[1]
                        k, m = n // NM, n % NM
                        if st[0] == "h":
                            ps = take(("h", f, n))
                            pe.matmul(ps[:, :], W1[:, k, m * P:(m + 1) * P], yT[:, :], start=True, stop=False)
                            fill(("h", f, n), pe.matmul(ps[:, :], maskw[:, n, :], Dm[:, :], start=False, stop=True))
                        else:
                            if m == 0:
                                ready(("sl", f))
                                ps = take(("o", f, k))
                                pe.matmul(ps[:, :], b2[:, k, :], sel[:, :], start=True, stop=False)
                            ps = bank[gb.slot[("o", f, k)][0]]
                            ready(("h", f, n))
                            ins = pe.matmul(ps[:, :], W2[:, k, m, :], Hb[:, n % 4, :], start=False, stop=(m == NM - 1))
                            ins.then_inc(h_used, 1)
                            if m == NM - 1:
                                pe.wait_ge(h_used, (b * 2 + f) * (NT * NM) + (n + 1))
                                pe.nop().then_inc(filled[gb.slot[("o", f, k)][0]], 1)
                    ready(("o", f, 2))
                    ps = take(("vt", f))
                    for c in range(HC):
                        ins = pe.transpose(ps[:, c * P:(c + 1) * P], FvT[:, c * P:(c + 1) * P], ident[:, :])
                    fill(("vt", f), ins)
                for f in range(2):
                    for k in range(2):
                        ready(("o", f, k))
                    ready(("vt", f))
                for st in attn2:
                    j = st[1]
                    if st[0] == "S":
                        a = st[2]
                        ps = take(st)
                        fill(st, pe.matmul(ps[:, :], F[:, 0, j * P:(j + 1) * P], F[:, 1, a * 512:(a + 1) * 512], start=True, stop=True))
                    elif st[0] == "T":
                        a = st[2]
                        ready(("S", j, a))
                        ps = take(st)
                        for k in range(4):
                            ins = pe.transpose(ps[:, k * P:(k + 1) * P], Pb[:, j % 3, (4 * a + k) * P:(4 * a + k + 1) * P], ident[:, :])
                        fill(st, ins)
                    else:
                        ps = take(st)
                        for a in range(2):
                            ready(("T", j, a))
                            for k in range(4):
                                ins = pe.matmul(ps[:, 0:D], PTb[:, (2 * j + a) % 4, k, :], Fv[:, 4 * a + k, :], start=(a + k == 0), stop=(4 * a + k == NC - 1))
                        ins.then_inc(av2_done, 1)
                        pe.wait_ge(av2_done, b * NC + (j + 1))
                        pe.nop().then_inc(filled[gb.slot[st][0]], 1)


def tree_constants(trees=3, depth=4, width=64):
    BIG = 2.0 ** 100
    nodes, leaves = 2 ** depth - 1, 2 ** depth
    path = np.zeros((96, P), np.float32)
    for k in range(trees):
        for leaf in range(leaves):
            cur = leaf + nodes
            while cur:
                parent, right = (cur - 1) // 2, (cur - 1) % 2
                if right:
                    path[32 * k + nodes + parent, 32 * k + leaf] = 1.0
                else:
                    path[32 * k + parent, 32 * k + leaf] = -1.0
                cur = parent
    pairs = leaves * width // P
    maskw = np.zeros((96, trees * pairs, P), np.float32)
    for k in range(trees):
        for m in range(pairs):
            for c in range(P):
                leaf = m * (P // width) + c // width
                maskw[:, k * pairs + m, c] = BIG * path[:, 32 * k + leaf] * 1.0
    comp = np.zeros((96, 1), np.float32)
    for k in range(trees):
        comp[32 * k + nodes:32 * k + 2 * nodes] = 1.0
    return {"c_maskw": maskw, "c_path": path, "c_comp": comp, "c_causal": np.triu(np.full((P, P), -BIG, np.float32), 1)}


def kernel(**inputs):
    import concourse.bacc as bacc
    from concourse.bass_utils import run_bass_kernel_spmd as run

    nc = bacc.Bacc("TRN2", target_bir_lowering=False, num_devices=1)
    arrays = {name: np.ascontiguousarray(a) for name, a in inputs.items()}
    arrays["c_ident"] = np.eye(P, dtype=np.float32)
    arrays["c_mask"] = np.triu(np.ones((P, P), np.float32))
    arrays.update(tree_constants())
    t = {}
    for name, a in arrays.items():
        t[name] = nc.dram_tensor(name, a.shape, mybir.dt.from_np(a.dtype), kind="ExternalInput").ap()
    shape = arrays["L0_attn_x"].shape
    t["out"] = nc.dram_tensor("out", shape, F32, kind="ExternalOutput").ap()
    t["x_mid"] = nc.dram_tensor("x_mid", (shape[0] * shape[1] // (4 * P) + 1, P, 4 * shape[2]), F32, kind="Internal").ap()
    build(nc, t)
    return run(nc, [arrays], core_ids=[0]).results[0]["out"]
```

```python
from contextlib import ExitStack
from itertools import chain

import numpy as np

import concourse.bass as bass
from concourse import mybir

F32 = mybir.dt.float32
F32R = mybir.dt.float32r
BF16 = mybir.dt.bfloat16
I32 = mybir.dt.int32
ALU = mybir.AluOpType
ACT = mybir.ActivationFunctionType
AX = mybir.AxisListType

P = 128
NBANK = 8
BIG = 2.0 ** 100
PRIMED = 1


class Groups:

    def __init__(self, names, before, undrained=(0,) * NBANK, held=(), held_banks=()):
        self.undrained = undrained
        self.slot, count = {}, [0] * NBANK
        rings = {False: [k for k in range(NBANK) if k not in held_banks], True: list(held_banks)}
        turn = {False: 0, True: 0}
        for name in names:
            own = name[0] in held
            k = rings[own][turn[own] % len(rings[own])]
            turn[own] += 1
            self.slot[name] = (k, count[k])
            count[k] += 1
        self.before, self.per = list(before), count

    def after(self, rounds):
        return [b + rounds * p for b, p in zip(self.before, self.per)]

    def filled(self, name, i):
        k, u = self.slot[name]
        return i * self.per[k] + (self.before[k] + u + 1)

    def free(self, name, i):
        k, u = self.slot[name]
        return i * self.per[k] + (self.before[k] - self.undrained[k] + u + PRIMED)

    def drained(self, name, i):
        return self.free(name, i) + 1


def build(nc, t):
    ctx = ExitStack()
    with ctx:
        bank = [ctx.enter_context(nc.psum_tensor(f"bank{k}", [P, 512], F32)) for k in range(NBANK)]
        filled = [ctx.enter_context(nc.semaphore(f"filled{k}")) for k in range(NBANK)]
        drained = [ctx.enter_context(nc.semaphore(f"drained{k}")) for k in range(NBANK)]
        ident = ctx.enter_context(nc.sbuf_tensor("ident", [P, P], F32))
        last = phase_a(nc, t, ctx, bank, filled, drained, ident)
        phase_b(nc, t, ctx, bank, filled, drained, last, ident)


RSQRT_STEPS = 10


def rsqrt_steps(dve, y, u, x):
    return [lambda: dve.tensor_scalar(u.bitcast(I32), x.bitcast(I32), 1, None, ALU.logical_shift_right),
            lambda: dve.tensor_scalar(y.bitcast(I32), u.bitcast(I32), -1.0, float(0x5F1FFFF9), ALU.mult, ALU.add),
            lambda: dve.tensor_tensor(u, y, y, ALU.mult),
            lambda: dve.scalar_tensor_tensor(u, u, -0.703952253, x, ALU.mult, ALU.mult),
            lambda: dve.scalar_tensor_tensor(y, u, 0.703952253 * 2.38924456, y, ALU.add, ALU.mult),
            lambda: dve.tensor_tensor(u, y, y, ALU.mult),
            lambda: dve.tensor_tensor(u, u, x, ALU.mult),
            lambda: dve.scalar_tensor_tensor(u, u, -10.0 / 3.0, u, ALU.add, ALU.mult),
            lambda: dve.tensor_scalar(u, u, 0.375, 1.875, ALU.mult, ALU.add),
            lambda: dve.tensor_tensor(y, y, u, ALU.mult)]


def round_of_phase_a(NM, NF, NS, NQ, PAIRS):
    steps = [("wo",)]
    steps += [(kind, m) for kind in "qk" for m in range(NM)]
    for n in range(NS * NQ + 4):
        if n == 0:
            steps += [("kt", 0, h) for h in range(2)]
        if n % NQ == 0 and n < NS * NQ:
            steps.append(("kbd", n // NQ))
        if n % NQ == 2 and n // NQ + 1 < NS:
            steps += [(kind, n // NQ + 1, h) for kind in ("v", "kt")[n < NQ:] for h in range(2)]
        if n < NS * NQ:
            steps.append(("sc", n))
        if 0 <= n - 2 < NS * NQ:
            steps.append(("av", n - 2))
            if (n - 2) % NQ == NQ - 1:
                steps += [("st", (n - 2) // NQ, r) for r in range(len(PAIRS))]
        if 0 <= n - 4 and (n - 4) % 2 == 1:
            steps.append(("tr", (n - 4) // 2))
    steps.append(("x1T",))
    tail = {("q", 2): [("v", 0, 0)], ("q", 4): [("v", 0, 1)], ("q", 6): [("v", 1, 0)], ("k", 0): [("v", 1, 1)],
            ("k", 3): [("x2T",)], ("k", 7): [("f1", m) for m in range(NF)], ("sc", 1): [("f2",)],
            ("sc", 7): [("x3T",)], ("sc", 8): [("w1", 0), ("w1", 1)], ("sc", 9): [("w1", 2), ("w1", 3)],
            ("sc", 12): [("hT", m) for m in range(NF)], ("sc", 13): [("w2",)]}
    out = []
    for st in steps:
        out.append(st)
        out += tail.get(st, [])
    return out


def phase_a(nc, t, ctx, bank, filled, drained, ident):
    NB, T, D = t["L0_attn_x"].shape
    H, DH, NS = 16, 64, 4
    HF = t["L0_attn_Wf1"].shape[1]
    NC, NG, NM, NF, NQ = T // P, NB // NS, H * DH // P, HF // P, H // 4
    N = NS * P
    W = DH + 1
    ROUND = 12582912.0
    PAIRS = [(0, 3), (3, 6), (6, 8)]
    ROUNDS = NG * NC
    steps = round_of_phase_a(NM, NF, NS, NQ, PAIRS)
    blocks = [(kind, m) for kind in "qk" for m in range(NM)]
    TAIL = ("wo", "x2T", "f1", "f2", "x3T", "w1", "hT", "w2")
    NOBANK = ("kbd",)
    KBD_ORDER = [(0, 0), (1, 0), (0, 1), (1, 1)] + [(s, half) for s in range(2, NS) for half in range(2)]
    setup = Groups([("wsum", 0), ("wsum", 1), ("wT", 0), ("wT", 1)], [0] * NBANK)
    first = Groups([("x1T",)], setup.after(1), setup.after(1))
    body = Groups([st for st in steps if st[0] not in NOBANK], first.after(1), setup.after(1))
    final = Groups([st for st in steps if st[0] in TAIL], body.after(ROUNDS), setup.after(1))

    with ExitStack() as stack:
        sb = lambda name, shape, dt=F32: stack.enter_context(nc.sbuf_tensor(name, shape, dt))
        sem = lambda name: ctx.enter_context(nc.semaphore(name))

        mask = sb("mask", [P, P])
        ones = sb("ones", [P, P])
        whi = sb("whi", [P, 3, H * DH], F32R)
        wlo = sb("wlo", [P, 3, H * DH], F32R)
        wo = sb("wo", [P, NM, D])
        wf1 = sb("wf1", [P, HF])
        wf2 = sb("wf2", [P, NF, D])
        w1T = sb("w1T", [P, HF])
        w2T = sb("w2T", [P, NF, D])
        lng = sb("lng", [P, 6])
        hln = sb("hln", [P, 2, NF])
        b1r = sb("b1r", [P, HF])
        b2r = sb("b2r", [P, D])

        xs = sb("xs", [P, NS, D])
        xr = sb("xr", [P, NS, D])
        xn = sb("xn", [P, NS, D])
        hT = sb("hT", [P, N])
        hhi = sb("hhi", [P, N], F32R)
        hlo = sb("hlo", [P, N], F32R)
        tmp = sb("tmp", [P, 4, N])
        QT = sb("QT", [P, NM, N])
        KT = sb("KT", [P, NM, N])
        KBD = sb("KBD", [P, 2, NM, 2, P])
        Ktok = sb("Ktok", [P, 2, H * DH])
        V = sb("V", [P, 2, NM, 2, 2 * W])
        S = sb("S", [P, NS, NM, 2 * W])
        PT = sb("PT", [P, 4, 4, P])
        AO = sb("AO", [P, 2, H * DH])
        rden = sb("rden", [P, 4, 4])

        x1 = sb("x1", [P, NS, D])
        x01 = sb("x01", [P, NS, D])
        xn2 = sb("xn2", [P, NS, D])
        xa = sb("xa", [P, NS, D])
        xo = sb("xo", [P, NS, D])
        hT2 = sb("hT2", [P, N])
        GT = sb("GT", [P, NF, N])
        hb = sb("hb", [P, NS, HF])
        bst = sb("bst", [P, 2, NS, 6])
        mv = sb("mv", [P, 2, NS, 2])
        rs = sb("rs", [P, 2, 4, NS])
        pad = sb("pad", [P, 1])
        prime = sb("prime", [P, NBANK + 2])

        w1raw, w2raw = hb[:, 0, :], hb[:, 1, :]
        wabs = rs[:, 1, 3, 0:4]
        wqkv_raw = QT[:, :, :].rearrange("p m n -> p (m n)")[:, 0:3 * H * DH].rearrange("p (w n) -> p w n", w=3)

        w_loaded, w2_loaded, wqkv_loaded = sem("w_loaded"), sem("w2_loaded"), sem("wqkv_loaded")
        wabs_ready, wq_ready, wT_ready = sem("wabs_ready"), sem("wq_ready"), sem("wT_ready")
        zeroed, whi_ready, split_w = sem("zeroed"), sem("whi_ready"), sem("split_w")
        x_loaded, x_used = sem("x_loaded"), sem("x_used")
        xn_ready, xn2_ready = sem("xn_ready"), sem("xn2_ready")
        hhi_ready, hlo_ready = sem("hhi_ready"), sem("hlo_ready")
        exp_ready, phi_ready = sem("exp_ready"), sem("phi_ready")
        kbd_ready = sem("kbd_ready")
        x01_ready = sem("x01_ready")
        state_ready = sem("state_ready")
        hact_ready, hn_ready = sem("hact_ready"), sem("hn_ready")
        xo_ready, xo_stored, xo_free = sem("xo_ready"), sem("xo_stored"), sem("xo_free")
        dve_step = sem("dve_step")

        block = stack.enter_context(nc.Block())

        def tile_of(ap, g, c):
            return ap.rearrange("b (c p) d -> p b c d", p=P)[:, bass.ds(g * NS, NS), bass.ds(c, 1), :] \
                .rearrange("p b c d -> p (b c) d")

        @block.sync
        def _(sp):
            for dst, src in ((w1raw.rearrange("p (m d) -> p m d", m=NF), t["L0_ffn_w1"].rearrange("(m p) d -> p m d", p=P)),
                             (w2raw, t["L0_ffn_w2"]), (ident[:, :], t["c_ident"]), (mask[:, :], t["c_mask"])):
                sp.dma_start(dst, src).then_inc(w_loaded, 16)
            for n, name in enumerate(("L0_attn_Wq", "L0_attn_Wk", "L0_attn_Wv")):
                sp.dma_start(wqkv_raw[:, n, :], t[name]).then_inc(wqkv_loaded, 16)
            with sp.Fori(0, NG) as g:
                with sp.Fori(0, NC) as c:
                    i = g * NC + c
                    sp.wait_ge(x_used, i + PRIMED)
                    sp.dma_start(xs[:, :, :], tile_of(t["L0_attn_x"], g, c)).then_inc(x_loaded, 16)
            sp.wait_ge(x_used, ROUNDS + PRIMED)
            sp.dma_start(xs[:, :, :], tile_of(t["L0_attn_x"], 0, 0)).then_inc(x_loaded, 16)
        W2_DMAS = 6 + 2 * NF + 3 + 2

        @block.gpsimd
        def _(pool):
            for n, primed in enumerate(drained + [x_used, xo_free]):
                pool.memset(prime[:, n:n + 1], 0.0).then_inc(primed, PRIMED)
            pool.memset(ones[:, :], 1.0).then_inc(zeroed, 1)
            pool.memset(KBD[:, :, :, :, :], 0.0).then_inc(zeroed, 1)
            pool.memset(S[:, :, :, :], 0.0).then_inc(zeroed, 1)
            pool.memset(xr[:, :, :], 0.0).then_inc(zeroed, 1)
            pool.memset(V[:, :, :, 0, W:2 * W], 0.0).then_inc(zeroed, 1)
            pool.memset(V[:, :, :, 1, 0:W], 0.0).then_inc(zeroed, 1)
            pool.memset(V[:, :, :, 0, DH:W], 1.0).then_inc(zeroed, 1)
            pool.memset(V[:, :, :, 1, 2 * W - 1:2 * W], 1.0).then_inc(zeroed, 1)
            pool.wait_ge(zeroed, 8)
            pool.wait_ge(whi_ready, 1)
            pool.tensor_tensor(wlo[:, :, :], wqkv_raw, whi[:, :, :].bitcast(F32), ALU.subtract).then_inc(split_w, 1)
            pool.wait_ge(split_w, 1)
            pool.memset(QT[:, :, :], 0.0).then_inc(split_w, 1)

            def low_part(n):
                pool.wait_ge(hhi_ready, n * 2 + 2)
                pool.tensor_tensor(hlo[:, :], hT[:, :], hhi[:, :].bitcast(F32), ALU.subtract).then_inc(hlo_ready, 1)

            low_part(0)

            def sums_of_residuals(grp, i):
                pool.wait_ge(drained[grp.slot[("wo",)][0]], grp.drained(("wo",), i))
                pool.tensor_tensor(x01[:, :, :], xr[:, :, :], x1[:, :, :], ALU.add).then_inc(x01_ready, 1)

            with pool.Fori(0, ROUNDS) as i:
                sums_of_residuals(body, i)
                pool.wait_ge(x01_ready, i + 1)
                for s, half in KBD_ORDER:
                    if s == 0:
                        name = ("k", 4 * half + 3)
                        pool.wait_ge(drained[body.slot[name][0]], body.drained(name, i))
                    if s >= 2 and half == 0:
                        name = ("sc", (s - 1) * NQ - 1)
                        pool.wait_ge(filled[body.slot[name][0]], body.filled(name, i))
                    ms = slice(4 * half, 4 * half + 4)
                    for h in range(2):
                        r = slice(h * DH, (h + 1) * DH)
                        pool.tensor_tensor(KBD[r, s % 2, ms, h, :], KT[r, ms, s * P:(s + 1) * P],
                                           KBD[r, s % 2, ms, 1 - h, :], ALU.add).then_inc(kbd_ready, 1)
                pool.wait_ge(kbd_ready, i * (4 * NS) + 4 * NS)
                low_part(i + 1)
                pool.wait_ge(xo_ready, i + 1)
                pool.dma_start(t["x_mid"][bass.ds(i, 1), :, :].rearrange("a p n -> (a p) n"),
                               xo[:, :, :].rearrange("p s d -> p (s d)")).then_inc(xo_stored, 16)
                pool.wait_ge(xo_stored, i * 16 + 16)
                pool.sem_inc(xo_free, 1)
            sums_of_residuals(final, 0)
            pool.wait_ge(xo_ready, ROUNDS + 1)
            pool.dma_start(t["x_mid"][ROUNDS, :, :], xo[:, :, :].rearrange("p s d -> p (s d)")).then_inc(xo_stored, 16)
            pool.wait_ge(xo_stored, 16 * (ROUNDS + 1))

        @block.scalar
        def _(act):
            act.wait_ge(w_loaded, 64)
            act.activation(tmp[:, 0, :], w1raw, ACT.Abs, accum_out=wabs[:, 0:1]).then_inc(wabs_ready, 1)
            act.activation(tmp[:, 1, :], w2raw, ACT.Abs, accum_out=wabs[:, 1:2]).then_inc(wabs_ready, 1)
            for n, name in enumerate(("L0_attn_ln1_g", "L0_attn_ln1_b", "L0_attn_ln2_g", "L0_attn_ln2_b", "L0_ffn_ln1_g", "L0_ffn_ln1_b")):
                act.dma_start(lng[:, n:n + 1], t[name].rearrange("(p a) -> p a", a=1)).then_inc(w2_loaded, 16)
            for n, name in enumerate(("L0_ffn_ln2_g", "L0_ffn_ln2_b")):
                for m in range(NF):
                    act.dma_start(hln[:, n, m:m + 1], t[name][m * P:(m + 1) * P].rearrange("(p a) -> p a", a=1)).then_inc(w2_loaded, 16)
            act.dma_start(wo[:, :, :], t["L0_attn_Wo"].rearrange("(m p) d -> p m d", p=P)).then_inc(w2_loaded, 16)
            act.dma_start(wf1[:, :], t["L0_attn_Wf1"]).then_inc(w2_loaded, 16)
            act.dma_start(wf2[:, :, :], t["L0_attn_Wf2"].rearrange("(m p) d -> p m d", p=P)).then_inc(w2_loaded, 16)
            act.dma_start(b1r[:, :], t["L0_ffn_b1"].rearrange("(a n) -> a n", a=1).broadcast_to([P, HF])).then_inc(w2_loaded, 16)
            act.dma_start(b2r[:, :], t["L0_ffn_b2"].rearrange("(a n) -> a n", a=1).broadcast_to([P, D])).then_inc(w2_loaded, 16)
            act.wait_ge(wqkv_loaded, 48)
            act.activation(whi[:, :, :], wqkv_raw, ACT.Copy).then_inc(whi_ready, 1)
            act.wait_ge(zeroed, 8)

            def run(steps, grp, i):
                def full(name):
                    act.wait_ge(filled[grp.slot[name][0]], grp.filled(name, i))
                    return bank[grp.slot[name][0]]

                def freed(name, ins):
                    ins.then_inc(drained[grp.slot[name][0]], 1)

                def affine(name, out, k):
                    return act.activation(out, full(name)[:, :], ACT.Identity, scale=lng[:, 2 * k:2 * k + 1], bias=lng[:, 2 * k + 1:2 * k + 2])

                for st in steps:
                    kind = st[0]
                    if kind == "x1T":
                        affine(st, hT[:, :], 0).then_inc(hhi_ready, 1)
                        freed(st, affine(st, hhi[:, :], 0))
                        act.wait_ge(drained[grp.slot[st][0]], grp.drained(st, i))
                        act.sem_inc(hhi_ready, 1)
                    elif kind in ("x2T", "x3T"):
                        freed(st, affine(st, hT2[:, :], 1 if kind == "x2T" else 2))
                    elif kind in "qk":
                        n = st[1] + NM * (kind == "k")
                        ps = full(st)
                        if n == 0:
                            full(("wo",))
                        if n == 3:
                            act.wait_ge(x01_ready, i + 1)
                            act.activation(xr[:, :, :], xs[:, :, :], ACT.Copy).then_inc(x_used, 1)
                        if n >= 4:
                            if n % 2 == 0:
                                act.wait_ge(phi_ready, i * NM + (n // 2 - 1))
                            else:
                                act.wait_ge(drained[grp.slot[blocks[n - 4]][0]], grp.drained(blocks[n - 4], i))
                        act.activation(tmp[:, n % 4, :], ps[:, :], ACT.Exp).then_inc(exp_ready, 1)
                        if n % 2 == 0:
                            dst = QT if kind == "q" else KT
                            freed(st, act.activation(dst[:, st[1], :], ps[:, :], ACT.Relu))
                    elif kind == "v":
                        _, s, h = st
                        ps = full(st)[:, :].rearrange("p (m h d) -> p m h d", h=2, d=DH)
                        act.activation(V[:, s % 2, 4 * h:4 * h + 4, 0, 0:DH], ps[:, :, 0, :], ACT.Copy)
                        freed(st, act.activation(V[:, s % 2, 4 * h:4 * h + 4, 1, W:W + DH], ps[:, :, 1, :], ACT.Copy))
                    elif kind == "kt":
                        _, s, h = st
                        freed(st, act.activation(Ktok[:, s % 2, 512 * h:512 * h + 512], full(st)[:, :], ACT.Copy))
                    elif kind == "tr":
                        s, half = st[1] // 2, st[1] % 2
                        freed(st, act.activation(QT[:, 4 * half:4 * half + 4, s * P:(s + 1) * P],
                                                 full(st)[:, :].rearrange("p (m q) -> p m q", q=P), ACT.Copy))
                    elif kind == "f1":
                        freed(st, act.activation(GT[:, st[1], :], full(st)[:, :], ACT.Gelu))
                    elif kind == "w1":
                        act.wait_ge(drained[grp.slot[st][0]], grp.drained(st, i))
                        act.activation(hb[:, st[1], :], hb[:, st[1], :], ACT.Gelu).then_inc(hact_ready, 1)
                    elif kind == "hT":
                        m = st[1]
                        freed(st, act.activation(GT[:, m, :], full(st)[:, :], ACT.Identity, scale=hln[:, 0, m:m + 1], bias=hln[:, 1, m:m + 1]))

            act.wait_ge(w2_loaded, 16 * W2_DMAS)
            run([("x1T",)], first, 0)
            with act.Fori(0, ROUNDS) as i:
                run(steps, body, i)
            run([st for st in steps if st[0] in TAIL], final, 0)

        @block.vector
        def _(dve):
            count, base = [0], [0]

            def step(ins):
                count[0] += 1
                ins.then_inc(dve_step, 1)
                return count[0]

            def settle(n=None):
                dve.wait_ge(dve_step, base[0] + (count[0] if n is None else n))

            def do(ins):
                step(ins)
                settle()

            def stats(src, k):
                for s in range(NS):
                    n = step(dve.bn_stats(bst[:, k, s, :], src[:, s, :]))
                    yield
                settle(n)
                dve.memset(pad[:, :], 0.0)
                for s in range(NS):
                    n = step(dve.bn_aggr(mv[:, k, s, :], bst[:, k, s, :]))
                yield
                settle(n)

            def rstds(var, k, out):
                y, u, x = rs[:, k, out, :], rs[:, k, 1, :], rs[:, k, 3, :]
                n = step(dve.tensor_scalar(x, var, 1e-5, None, ALU.add))
                yield
                for ins in rsqrt_steps(dve, y, u, x):
                    settle(n)
                    n = step(ins())
                    yield
                settle(n)

            def normalise(src, dst, k, out, ready):
                for s in range(NS):
                    ins = dve.tensor_scalar(dst[:, s, :], src[:, s, :], mv[:, k, s, 0:1], rs[:, k, out, s:s + 1], ALU.subtract, ALU.mult)
                    if s < NS - 1 or ready is None:
                        step(ins)
                    else:
                        ins.then_inc(ready, 1)
                    yield

            def layernorm(src, dst, ready, k):
                yield from stats(src, k)
                yield from rstds(mv[:, k, :, 1], k, 0)
                yield from normalise(src, dst, k, 0, ready)

            dve.wait_ge(x_loaded, 16)
            for _ in layernorm(xs, xn, xn_ready, 0):
                pass
            dve.wait_ge(w_loaded, 64)
            for j, wraw in enumerate((w1raw, w2raw)):
                k = setup.slot[("wsum", j)][0]
                dve.wait_ge(filled[k], setup.filled(("wsum", j), 0))
                sc, inv = rs[:, 1, 2, 2 * j:2 * j + 1], rs[:, 1, 2, 2 * j + 1:2 * j + 2]
                do(dve.tensor_scalar(sc, bank[k][:, 0:1], 1.0 / (HF * D), 1e-5, ALU.mult, ALU.max))
                do(dve.reciprocal(sc, sc))
                do(dve.reciprocal(inv, sc))
                q = tmp[:, j, :]
                do(dve.tensor_scalar(q, wraw, sc, 2.0, ALU.mult, ALU.min))
                do(dve.tensor_scalar(q, q, -2.0, ROUND, ALU.max, ALU.add))
                do(dve.tensor_scalar(q, q, ROUND, 1.0, ALU.subtract, ALU.min))
                do(dve.tensor_scalar(q, q, -1.0, inv, ALU.max, ALU.mult))
                do(dve.tensor_tensor(q, q, wraw, ALU.subtract))
                dve.tensor_tensor(q, wraw, q, ALU.add).then_inc(wq_ready, 1)
                k = setup.slot[("wT", j)][0]
                dve.wait_ge(filled[k], setup.filled(("wT", j), 0))
                dst = w1T[:, :] if j == 0 else w2T[:, :, :].rearrange("p m d -> p (m d)")
                dve.tensor_copy(dst, bank[k][:, :]).then_inc(wT_ready, 1)
            dve.wait_ge(wT_ready, 2)
            dve.wait_ge(w2_loaded, 16 * W2_DMAS)
            dve.wait_ge(split_w, 2)
            dve.wait_ge(zeroed, 8)
            setup_steps = count[0]

            def run(steps, grp, i, late):
                weaving = [iter(()), iter(())]
                turn = [0]

                def weave(n):
                    for _ in range(n):
                        turn[0] = 1 - turn[0]
                        if next(weaving[turn[0]], True):
                            next(weaving[1 - turn[0]], None)

                def finish(lane=0):
                    for _ in weaving[lane]:
                        pass

                def full(name):
                    dve.wait_ge(filled[grp.slot[name][0]], grp.filled(name, i))
                    return bank[grp.slot[name][0]]

                def written(name):
                    dve.wait_ge(drained[grp.slot[name][0]], grp.drained(name, i))

                def freed(name, ins):
                    ins.then_inc(drained[grp.slot[name][0]], 1)

                def after_wo():
                    yield from layernorm(x1, xn2, xn2_ready, 1)

                def after_f2():
                    yield from stats(x01, 1)
                    yield from rstds(mv[:, 1, :, 1], 1, 0)
                    r, r2, u = rs[:, 1, 0, :], rs[:, 1, 2, :], rs[:, 1, 1, :]
                    n = step(dve.tensor_tensor(u, r, r, ALU.mult))
                    yield
                    settle(n)
                    n = step(dve.tensor_tensor(u, u, mv[:, 1, :, 1], ALU.mult))
                    yield
                    settle(n)
                    yield from rstds(u, 1, 2)
                    n = step(dve.tensor_tensor(r2, r2, r, ALU.mult))
                    yield
                    settle(n)
                    yield from normalise(x01, xn2, 1, 2, xn2_ready)
                    yield from normalise(x01, xa, 1, 0, None)

                def after_w1():
                    dve.wait_ge(hact_ready, late * NS + NS)
                    yield from layernorm(hb, hb, hn_ready, 1)

                def after_w2():
                    settle()
                    n = step(dve.tensor_tensor(x1[:, :, :], xa[:, :, :], x1[:, :, :], ALU.add))
                    yield
                    settle(n)
                    dve.wait_ge(xo_free, late + PRIMED)
                    yield from layernorm(x1, xo, xo_ready, 1)

                def next_tile():
                    dve.wait_ge(x_loaded, i * 16 + 32)
                    yield from layernorm(xs, xn, xn_ready, 0)

                tokens = lambda ap: ap[:, :].rearrange("p (s d) -> p s d", d=D)
                for st in steps:
                    kind = st[0]
                    if kind == "wo":
                        ps = full(st)
                        dve.wait_ge(x_used, late + PRIMED)
                        freed(st, dve.tensor_tensor(x1[:, :, :], xr[:, :, :], tokens(ps), ALU.add))
                        written(st)
                        weaving[0] = after_wo()
                    elif kind in ("x2T", "x3T"):
                        finish()
                    elif kind == "x1T":
                        finish(1)
                    elif kind in "qk":
                        n = st[1] + NM * (kind == "k")
                        e, dst = tmp[:, n % 4, :], (QT if kind == "q" else KT)[:, st[1], :]
                        if n % 2 == 0:
                            written(st)
                            dve.scalar_tensor_tensor(dst, e, 1.0, dst, ALU.min, ALU.add).then_inc(phi_ready, 1)
                        else:
                            dve.wait_ge(exp_ready, i * (2 * NM) + (n + 1))
                            k = step(dve.tensor_scalar(e, e, 1.0, None, ALU.min))
                            weave(2)
                            settle(k)
                            freed(st, dve.scalar_tensor_tensor(dst, full(st)[:, :], 0.0, e, ALU.max, ALU.add))
                        weave(2)
                    elif kind == "sc":
                        n = st[1]
                        ps = full(st)
                        freed(st, dve.tensor_tensor(PT[:, n % 4, :, :], ps[:, :].rearrange("p (h q) -> p h q", q=P),
                                                    mask[:, :].unsqueeze(1).broadcast_to([P, 4, P]), ALU.mult))
                        weave(5)
                        if n == 2:
                            weaving[1] = next_tile()
                    elif kind == "av":
                        n = st[1]
                        s, q = n // NQ, n % NQ
                        ps = full(st)[:, 0:4 * W].rearrange("p (h w) -> p h w", w=W)
                        r = rden[:, n % 4, :]
                        k = step(dve.tensor_scalar(r, ps[:, :, DH], 1e-6, None, ALU.max))
                        weave(2)
                        settle(k)
                        k = step(dve.reciprocal(r, r))
                        weave(1)
                        settle(k)
                        freed(st, dve.tensor_tensor(AO[:, s % 2, q * 256:(q + 1) * 256].rearrange("p (h d) -> p h d", d=DH),
                                                    ps[:, :, 0:DH], r.unsqueeze(2).broadcast_to([P, 4, DH]), ALU.mult))
                        weave(3)
                    elif kind == "st":
                        _, s, r = st
                        a, b = PAIRS[r]
                        ps = full(st)[:, 0:(b - a) * 2 * W].rearrange("p (m w) -> p m w", w=2 * W)
                        for h in range(2):
                            rows, cols = slice(h * DH, (h + 1) * DH), slice(h * W, (h + 1) * W)
                            ins = dve.tensor_tensor(S[rows, s, a:b, cols], S[rows, s, a:b, cols], ps[rows, :, cols], ALU.add)
                        freed(st, ins)
                        weave(1)
                    elif kind == "f2":
                        ps = full(st)
                        dve.wait_ge(x01_ready, late + 1)
                        freed(st, dve.tensor_tensor(x01[:, :, :], x01[:, :, :], tokens(ps), ALU.add))
                        written(st)
                        weaving[0] = after_f2()
                    elif kind == "w1":
                        ps = full(st)
                        freed(st, dve.tensor_tensor(hb[:, st[1], :], ps[:, :], b1r[:, :], ALU.add))
                        if st[1] == NS - 1:
                            weaving[0] = after_w1()
                    elif kind == "hT" and st[1] == 0:
                        finish()
                    elif kind == "w2":
                        ps = full(st)
                        freed(st, dve.tensor_tensor(x1[:, :, :], tokens(ps), b2r[:, :].unsqueeze(1).broadcast_to([P, NS, D]), ALU.add))
                        written(st)
                        weaving[0] = after_w2()
                finish()
                dve.wait_ge(xo_ready, late + 1)
                if grp is body:
                    written(("st", NS - 1, len(PAIRS) - 1))

            RSTD = 1 + RSQRT_STEPS
            LN = 2 * NS + RSTD + NS - 1
            DVE_ROUND = 5 * LN + (RSTD + 3 + NS) + 1 + 2 * NS * NQ + NM
            with dve.Fori(0, NG) as g:
                dve.memset(S[0:DH, :, :, 0:W], 0.0).then_inc(state_ready, 1)
                dve.memset(S[DH:P, :, :, W:2 * W], 0.0).then_inc(state_ready, 1)
                dve.wait_ge(state_ready, g * 2 + 2)
                dve.memset(pad[:, :], 0.0)
                with dve.Fori(0, NC) as c:
                    i = g * NC + c
                    base[0], count[0] = i * DVE_ROUND + setup_steps, 0
                    run(steps, body, i, i)
                    assert count[0] == DVE_ROUND, count[0]
            base[0], count[0] = ROUNDS * DVE_ROUND + setup_steps, 0
            run([st for st in steps if st[0] in TAIL], final, 0, ROUNDS)

        @block.tensor
        def _(pe):
            pe.wait_ge(zeroed, 1)
            pe.wait_ge(w_loaded, 64)
            pe.wait_ge(wabs_ready, 2)
            for j in range(2):
                k = setup.slot[("wsum", j)][0]
                pe.matmul(bank[k][:, 0:1], ones[:, :], wabs[:, j:j + 1], start=True, stop=True).then_inc(filled[k], 1)
            for j in range(2):
                pe.wait_ge(wq_ready, j + 1)
                k = setup.slot[("wT", j)][0]
                for m in range(NF):
                    ins = pe.transpose(bank[k][:, m * P:(m + 1) * P], tmp[:, j, m * P:(m + 1) * P], ident[:, :])
                ins.then_inc(filled[k], 1)
            pe.wait_ge(wT_ready, 2)
            pe.wait_ge(split_w, 2)
            pe.wait_ge(zeroed, 8)

            def run(steps, grp, i, g, late, tile):
                def take(name):
                    k = grp.slot[name][0]
                    pe.wait_ge(drained[k], grp.free(name, i))
                    return bank[k]

                def fill(name, ins):
                    ins.then_inc(filled[grp.slot[name][0]], 1)

                def ready(name):
                    k = grp.slot[name][0]
                    pe.wait_ge(drained[k], grp.drained(name, i))

                def transposes(name, x):
                    ps = take(name)
                    for s in range(NS):
                        ins = pe.transpose(ps[:, s * P:(s + 1) * P], x[:, s, :], ident[:, :])
                    fill(name, ins)

                for st in steps:
                    kind = st[0]
                    if kind == "wo":
                        ps = take(st)
                        for s in range(NS):
                            for m in range(NM):
                                ins = pe.matmul(ps[:, s * P:(s + 1) * P], QT[:, m, s * P:(s + 1) * P], wo[:, m, :], start=(m == 0), stop=(m == NM - 1))
                        fill(st, ins)
                    elif kind == "x1T":
                        pe.wait_ge(xn_ready, tile + 1)
                        transposes(st, xn)
                    elif kind in "qk":
                        w, m = "qk".index(kind), slice(st[1] * P, (st[1] + 1) * P)
                        if st == ("q", 0):
                            pe.wait_ge(hlo_ready, i + 1)
                        ps = take(st)
                        pe.matmul(ps[:, :], whi[:, w, m], hhi[:, :], start=True, stop=False)
                        pe.matmul(ps[:, :], whi[:, w, m], hlo[:, :], start=False, stop=False)
                        fill(st, pe.matmul(ps[:, :], wlo[:, w, m], hhi[:, :], start=False, stop=True))
                    elif kind == "v":
                        _, s, h = st
                        ps = take(st)
                        tok, cols = slice(s * P, (s + 1) * P), slice(h * 512, (h + 1) * 512)
                        pe.matmul(ps[:, :], hhi[:, tok], whi[:, 2, cols], start=True, stop=False)
                        pe.matmul(ps[:, :], hhi[:, tok], wlo[:, 2, cols], start=False, stop=False)
                        fill(st, pe.matmul(ps[:, :], hlo[:, tok], whi[:, 2, cols], start=False, stop=True))
                    elif kind == "kt":
                        _, s, h = st
                        if s == 0 and h == 0:
                            ready(("k", NM - 1))
                        ps = take(st)
                        for m in range(4):
                            ins = pe.transpose(ps[:, m * P:(m + 1) * P], KT[:, 4 * h + m, s * P:(s + 1) * P], ident[:, :])
                        fill(st, ins)
                    elif kind == "kbd":
                        s = st[1]
                        pe.wait_ge(kbd_ready, i * (4 * NS) + 2 * (KBD_ORDER.index((s, 0)) + 1))
                        if s == 0:
                            pe.wait_ge(state_ready, g * 2 + 2)
                    elif kind == "sc":
                        n = st[1]
                        s, q = n // NQ, n % NQ
                        if q == NQ // 2:
                            pe.wait_ge(kbd_ready, i * (4 * NS) + 2 * (KBD_ORDER.index((s, 1)) + 1))
                        ps = take(st)
                        for h in range(4):
                            m = 2 * q + h // 2
                            ins = pe.matmul(ps[:, h * P:(h + 1) * P], KBD[:, s % 2, m, h % 2, :], QT[:, m, s * P:(s + 1) * P], start=True, stop=True)
                        fill(st, ins)
                    elif kind == "av":
                        n = st[1]
                        s, q = n // NQ, n % NQ
                        ready(("sc", n))
                        if q == 0:
                            ready(("v", s, 1))
                        ps = take(st)
                        for j in range(2):
                            m = 2 * q + j
                            out = ps[:, 2 * j * W:2 * (j + 1) * W]
                            pe.matmul(out, QT[:, m, s * P:(s + 1) * P], S[:, s, m, :], start=True, stop=False, skip_group_check=True)
                            for h in range(2):
                                ins = pe.matmul(out, PT[:, n % 4, 2 * j + h, :], V[:, s % 2, m, h, :], start=False, stop=(h == 1), skip_group_check=True)
                        fill(st, ins)
                    elif kind == "st":
                        _, s, r = st
                        a, b = PAIRS[r]
                        if r == 0:
                            ready(("kt", s, 1))
                        ps = take(st)
                        for m in range(a, b):
                            both = V[:, s % 2, m, :, :].rearrange("p h w -> p (h w)")
                            both = both[:, 0:4 * W].rearrange("p (k w) -> p k w", w=W)[:, 0:4:3, :]
                            ins = pe.matmul(ps[:, (m - a) * 2 * W:(m - a + 1) * 2 * W], Ktok[:, s % 2, m * P:(m + 1) * P], both, start=True, stop=True)
                        fill(st, ins)
                    elif kind == "tr":
                        s, half = st[1] // 2, st[1] % 2
                        ready(("av", 4 * s + 2 * half + 1))
                        ps = take(st)
                        for m in range(4):
                            ins = pe.transpose(ps[:, m * P:(m + 1) * P], AO[:, s % 2, (4 * half + m) * P:(4 * half + m + 1) * P], ident[:, :])
                        fill(st, ins)
                    elif kind in ("x2T", "x3T"):
                        pe.wait_ge(xn2_ready, late * 2 + (1 if kind == "x2T" else 2))
                        transposes(st, xn2)
                    elif kind == "f1":
                        m = st[1]
                        if m == 0:
                            ready(("x2T",))
                        ps = take(st)
                        fill(st, pe.matmul(ps[:, :], wf1[:, m * P:(m + 1) * P], hT2[:, :], start=True, stop=True))
                    elif kind in ("f2", "w2"):
                        ready(("f1" if kind == "f2" else "hT", NF - 1))
                        w = wf2 if kind == "f2" else w2T
                        ps = take(st)
                        for s in range(NS):
                            for m in range(NF):
                                ins = pe.matmul(ps[:, s * P:(s + 1) * P], GT[:, m, s * P:(s + 1) * P], w[:, m, :], start=(m == 0), stop=(m == NF - 1))
                        fill(st, ins)
                    elif kind == "w1":
                        s = st[1]
                        if s == 0:
                            ready(("x3T",))
                        ps = take(st)
                        fill(st, pe.matmul(ps[:, :], hT2[:, s * P:(s + 1) * P], w1T[:, :], start=True, stop=True))
                    elif kind == "hT":
                        m = st[1]
                        if m == 0:
                            pe.wait_ge(hn_ready, late + 1)
                        ps = take(st)
                        for s in range(NS):
                            ins = pe.transpose(ps[:, s * P:(s + 1) * P], hb[:, s, m * P:(m + 1) * P], ident[:, :])
                        fill(st, ins)
                if grp is body:
                    ready(("tr", 2 * NS - 1))

            run([("x1T",)], first, 0, None, None, 0)
            with pe.Fori(0, NG) as g:
                with pe.Fori(0, NC) as c:
                    i = g * NC + c
                    run(steps, body, i, g, i, i + 1)
            run([st for st in steps if st[0] in TAIL], final, 0, None, ROUNDS, None)
    return final.after(1), setup.after(1)


def phase_b(nc, t, ctx, bank, filled, drained, last, ident):
    NB, T, D = t["L0_attn_x"].shape
    NC = T // P
    NH, KV, HD = 4, 2, 32
    SIDE = t["x_mid"].shape[2] // D
    NT, NL, LW = 3, 16, 64
    NM = NL * LW // P
    HC = NC // 2
    TREES = "qkv"

    units = [(j, h) for j in range(NC) for h in range(NH)]
    NU = len(units)

    def pieces(j):
        return [(a, min(4, j + 1 - a)) for a in range(0, j + 1, 4)]

    attn1 = []
    for u in range(NU + 7):
        if u < NU:
            attn1 += [("s", u, a) for a, _ in pieces(units[u][0])]
        if 0 <= u - 2 < NU:
            attn1 += [("t", u - 2, a) for a, _ in pieces(units[u - 2][0])]
        if 0 <= u - 4 < NU:
            attn1.append(("av", u - 4))
        if 0 <= u - 6 < NU and units[u - 6][1] == NH - 1:
            j = units[u - 6][0]
            attn1 += [("yT", 0)] * (j == NC - 1) + [("at", j)]
            if j % HC == HC - 1:
                attn1.append(("wo", j // HC))
    attn1.append(("nd", 0))
    front = [("xT", a) for a in range(2)] + [("qkv", r) for r in range(NC // 2)]
    front += [("qt", c) for c in range(NC)] + [("kt", r) for r in range(NC // 2)]
    between = {(0, 12): front[0:2], (0, 14): front[2:4], (0, 16): front[4:6],
               (0, 20): [("yT", 1)], (0, 21): [("nd", 1)], (0, 24): [("sl", 1)],
               (0, 1): [("sl", 0)], (1, 1): [("vt", 0)]}
    for k in range(6):
        between[1, 16 + k] = front[6 + 2 * k:8 + 2 * k]
    fff = []
    for f in range(2):
        for n in range(NT * NM + 3):
            if n < NT * NM:
                fff.append(("h", f, n))
            if n >= 3:
                fff.append(("o", f, n - 3))
            fff += between.get((f, n), [])
    attn2 = []
    for j in range(NC + 2):
        if j < NC:
            attn2 += [("S", j, a) for a in range(2)]
            if j == 0:
                attn2.append(("vt", 1))
        if 0 <= j - 1 < NC:
            attn2 += [("T", j - 1, a) for a in range(2)]
        if 0 <= j - 2 < NC:
            attn2.append(("A", j - 2))

    steps = attn1 + fff + attn2
    order = []
    for st in steps:
        if st[0] == "av":
            j, h = units[st[1]]
            if h == 0:
                order.append(("av", j))
        elif st[0] == "o":
            if st[2] % NM == 0:
                order.append(("o", st[1], st[2] // NM))
        else:
            order.append(st)
    before, undrained = last
    first = Groups(front, before, undrained, held=("av", "o"), held_banks=(6, 7))
    pre = Groups([("pre", 0), ("pre", 1)], first.after(1), undrained)
    undrained = [a + b for a, b in zip(undrained, pre.per)]
    gb = Groups(order, pre.after(1), undrained, held=("av", "o"), held_banks=(6, 7))
    tgroups = [st for st in attn1 if st[0] == "t"]
    tindex = {st: n for n, st in enumerate(tgroups)}
    SOFT = 1.0 / np.sqrt(np.float32(D))

    with ExitStack() as stack:
        sb = lambda name, shape, dt=F32: stack.enter_context(nc.sbuf_tensor("b_" + name, shape, dt))
        sem = lambda name: ctx.enter_context(nc.semaphore("b_" + name))

        wqkv = sb("wqkv", [P, 2 * D])
        wo = sb("wo", [P, D])
        normw = sb("normw", [P, 1])
        scal = sb("scal", [P, 4])
        W1hi = sb("W1hi", [P, NT, NL * LW], F32R)
        W1lo = sb("W1lo", [P, NT, NL * LW], F32R)
        W2hi = sb("W2hi", [P, NT, NM, D], F32R)
        W2lo = sb("W2lo", [P, NT, NM, D], F32R)
        b1raw = sb("b1raw", [NT * NM, P])
        b1 = sb("b1", [P, NT * NM])
        nwraw = sb("nwraw", [96, D])
        nwT = sb("nwT", [P, 96])
        nthr = sb("nthr", [96, 2])
        b2 = sb("b2", [P, NT, D])
        b2hi = sb("b2hi", [P, NT, D], F32R)
        b2lo = sb("b2lo", [P, NT, D], F32R)
        maskw = sb("maskw", [96, NT * NM, P], BF16)
        path = sb("path", [96, P], BF16)
        identb = sb("identb", [P, P], BF16)
        causal = sb("causal", [P, P], BF16)

        X = sb("X", [P, NC, D])
        Y = sb("Y", [P, NC, D])
        O = sb("O", [P, NC, D])
        QS = sb("QS", [P, NC, NH, 4, HD])
        KS = sb("KS", [P, NC, KV, 4, HD])
        QST = sb("QST", [P, NC, NH, P], F32R)
        KST = sb("KST", [P, KV, T], F32R)
        V = sb("V", [P, NC, 96])
        Pb = sb("Pb", [P, 3, T])
        PTb = sb("PTb", [P, 4, 4, P])
        AO = sb("AO", [P, 2, D])
        AOT = sb("AOT", [P, T])
        mx = sb("mx", [P, 4, 2])
        nb = sb("nb", [P, 4])
        sums = sb("sums", [P, 2, NH, 2])
        rsum = sb("rsum", [P, 2, NH])
        yT = sb("yT", [P, 4 * P])
        yhi = sb("yhi", [P, 2, 4 * P], F32R)
        ylo = sb("ylo", [P, 2, 4 * P], F32R)
        Dm = sb("Dm", [96, 2, 4 * P], BF16)
        sel = sb("sel", [P, 4 * P], F32R)
        Hhi = sb("Hhi", [P, 4, 4 * P], F32R)
        Hlo = sb("Hlo", [P, 4, 4 * P], F32R)
        F = sb("F", [P, 2, T])
        Fv = sb("Fv", [P, NC, D])
        pad = sb("pad", [P, 1])
        prime = sb("prime", [P, NBANK + 2])
        bst = sb("bst", [P, NC, 6])
        mv = sb("mv", [P, NC, 2])
        rs = sb("rs", [P, 4, 48])

        xn, hT = O, AOT
        Hb = Pb[:, :, :].rearrange("p a n -> p (a n)")[:, NC * 6 * HD:NC * 6 * HD + 8 * P].rearrange("p (a n) -> p a n", a=2)
        FvT = Pb[:, :, :].rearrange("p a n -> p (a n)")[:, NC * 6 * HD + 8 * P:NC * 6 * HD + 12 * P]
        PT_places = [PTb[:, n, :, :].rearrange("p k q -> p (k q)") for n in range(4)]
        PT_places += [F[:, n // 2, n % 2 * 512:(n % 2 + 1) * 512] for n in range(4)]
        W1raw = [F[:, 0, :], F[:, 1, :], Y[:, :, :].rearrange("p c d -> p (c d)")]
        W2raw = [PTb[:, 0:2, :, :].rearrange("p n k q -> p (n k) q"), PTb[:, 2:4, :, :].rearrange("p n k q -> p (n k) q"), Fv[:, :, :]]
        sq = QS[:, :, :, :, :].rearrange("p c h a d -> p (c h a d)")[:, 0:NC * 6 * HD].rearrange("p (c n) -> p c n", c=NC)
        QN = Pb[:, :, :].rearrange("p a n -> p (a n)")[:, 0:NC * 6 * HD].rearrange("p (c h d) -> p c h d", c=NC, d=HD)

        w_loaded, zeroed, pre_ready = sem("w_loaded"), sem("zeroed"), sem("pre_ready")
        late_loaded = sem("late_loaded")
        x_loaded, x_used = sem("x_loaded"), sem("x_used")
        xn_ready, sq_ready = sem("xn_ready"), sem("sq_ready")
        split_ready = sem("split_ready")
        nb_ready, p_ready, av_done = sem("nb_ready"), sem("p_ready"), sem("av_done")
        y_ready, out_ready = sem("y_ready"), sem("out_ready")
        out_stored, out_free = sem("out_stored"), sem("out_free")
        nb2_ready, p2_ready, av2_done = sem("nb2_ready"), sem("p2_ready"), sem("av2_done")
        h_used, hi_ready, y_lo_ready = sem("h_used"), sem("hi_ready"), sem("y_lo_ready")
        lo_ready = [sem("lo_ready0"), sem("lo_ready1")]
        dve_step, act_step = sem("dve_step"), sem("act_step")

        block = stack.enter_context(nc.Block())
        column = lambda ap: ap.rearrange("(p a) -> p a", a=1)
        wide_path, wide_causal = yT[0:96, 0:P], yT[:, P:2 * P]
        loads = [(wqkv[:, 0:D], t["L1_attn_Wq"]), (wqkv[:, D:D + 64], t["L1_attn_Wk"]), (wqkv[:, D + 64:], t["L1_attn_Wv"]),
                 (wo[:, :], t["L1_attn_Wo"]), (normw[:, :], column(t["L1_attn_norm_w"])),
                 (scal[:, 0:1], t["L1_attn_gate"].rearrange("(p a) -> p a", a=1).broadcast_to([P, 1])),
                 (scal[:, 1:2], t["L1_attn_log_temperature"].rearrange("(p a) -> p a", a=1).broadcast_to([P, 1])),
                 ]
        late_loads = [(wide_path, t["c_path"]), (wide_causal, t["c_causal"]), (nthr[:, 1:2], t["c_comp"])]
        for n, k in enumerate(TREES):
            late_loads += [(W1raw[n].rearrange("p (l h) -> p l h", l=NL), t[f"L1_ffn_{k}_w1"].rearrange("l d h -> d l h")),
                      (W2raw[n], t[f"L1_ffn_{k}_w2"].rearrange("(m a) h d -> (a h) m d", a=2)),
                      (b1raw[n * NM:(n + 1) * NM, :], t[f"L1_ffn_{k}_b1"].rearrange("(m a) h -> m (a h)", a=2))]
            for a in range(2):
                r = 32 * n + (NL - 1) * a
                late_loads += [(nwraw[r:r + NL - 1, :], t[f"L1_ffn_{k}_node_w"]), (nthr[r:r + NL - 1, 0:1], column(t[f"L1_ffn_{k}_node_b"]))]
            late_loads.append((b2[32 * n:32 * n + NL, n, :], t[f"L1_ffn_{k}_b2"]))

        def full(eng, name, b, grp=gb):
            k = grp.slot[name][0]
            eng.wait_ge(filled[k], grp.filled(name, b))
            return bank[k]

        def freed(name, ins, grp=gb):
            ins.then_inc(drained[grp.slot[name][0]], 1)

        def evacuated(eng, name, b, grp=gb):
            eng.wait_ge(drained[grp.slot[name][0]], grp.drained(name, b))

        def copy_transposed(eng, st, b):
            n = tindex[st]
            if n >= len(PT_places):
                eng.wait_ge(av_done, b * NU + (tgroups[n - len(PT_places)][1] + 1))
            ps = full(eng, st, b)
            w = dict(pieces(units[st[1]][0]))[st[2]]
            dst = PT_places[n % len(PT_places)][:, 0:w * P]
            if n % 2:
                freed(st, eng.activation(dst, ps[:, 0:w * P], ACT.Copy))
            else:
                freed(st, eng.tensor_copy(dst, ps[:, 0:w * P]))

        def hidden_low_part(eng, f, n, b):
            evacuated(eng, ("h", f, n), b)
            eng.tensor_tensor(Hlo[:, n % 4, :], Hb[:, n % 2, :], Hhi[:, n % 4, :].bitcast(F32), ALU.subtract).then_inc(lo_ready[n % 2], 1)

        split_weights = []
        for n in range(NT):
            split_weights += [(W1hi[:, n, :], W1raw[n], W1lo[:, n, :]), (W2hi[:, n, :, :], W2raw[n], W2lo[:, n, :, :])]
        split_weights.append((b2hi[:, :, :], b2[:, :, :], b2lo[:, :, :]))
        PREPARED = 1 + NT + 3 + 2 + len(split_weights)

        @block.sync
        def _(sp):
            for dst, src in loads:
                sp.dma_start(dst, src).then_inc(w_loaded, 16)
            with sp.Fori(0, NB // SIDE) as g:
                with sp.Fori(0, SIDE) as s:
                    sp.wait_ge(x_used, g * (2 * SIDE) + s * 2 + PRIMED)
                    sp.dma_start(X[:, :, :], t["x_mid"][bass.ds(g * NC + 1, NC), :, bass.ds(s * D, D)]
                                 .rearrange("c p d -> p c d")).then_inc(x_loaded, 16)
            sp.wait_ge(x_used, 2 * NB + PRIMED)
            sp.dma_start(X[:, :, :], t["x_mid"][1:NC + 1, :, 0:D].rearrange("c p d -> p c d")).then_inc(x_loaded, 16)

        @block.gpsimd
        def _(pool):
            for n, primed in enumerate((x_used, out_free)):
                pool.memset(prime[:, n:n + 1], 0.0).then_inc(primed, PRIMED)
            pool.memset(nwraw[:, :], 0.0).then_inc(zeroed, 1)
            pool.memset(nthr[:, :], 0.0).then_inc(zeroed, 1)
            pool.memset(b2[:, :, :], 0.0).then_inc(zeroed, 1)
            pool.memset(b1raw[:, :], 0.0).then_inc(zeroed, 1)
            pool.memset(V[:, :, 64:96], 0.0).then_inc(zeroed, 1)
            with pool.Fori(0, NB) as b:
                for f in range(2):
                    for n in range(1, NT * NM, 2):
                        hidden_low_part(pool, f, n, b)
                for a in range(2):
                    pool.wait_ge(out_ready, b * 2 + (a + 2))
                    pool.dma_start(t["out"].rearrange("b (c p) d -> b p c d", p=P)[bass.ds(b, 1), :, a * HC:(a + 1) * HC, :]
                                   .rearrange("b p c d -> p (b c) d"), O[:, a * HC:(a + 1) * HC, :]).then_inc(out_stored, 16)
                pool.wait_ge(out_stored, b * 32 + 32)
                pool.sem_inc(out_free, 1)

        @block.scalar
        def _(act):
            act.wait_ge(zeroed, 5)
            for dst, src in late_loads:
                act.dma_start(dst, src).then_inc(late_loaded, 16)
            act.wait_ge(w_loaded, 16 * len(loads))
            act.activation(scal[:, 2:3], scal[:, 1:2], ACT.Exp).then_inc(act_step, 1)
            act.wait_ge(act_step, 1)
            act.activation(scal[:, 3:4], scal[:, 2:3], ACT.Copy, scale=-1.0).then_inc(pre_ready, 1)

            def front_step(st, grp, b, seq):
                kind, k = st
                if kind == "xT":
                    freed(st, act.activation(hT[:, k * 512:(k + 1) * 512], full(act, st, b, grp)[:, :], ACT.Copy, scale=normw[:, 0:1]), grp)
                elif kind == "qkv":
                    ps = full(act, st, b, grp)[:, :].rearrange("p (c n) -> p c n", c=2)
                    act.activation(sq[:, 2 * k:2 * k + 2, :], ps[:, :, 0:192], ACT.Square)
                    act.activation(QN[:, 2 * k:2 * k + 2, :, :].rearrange("p c h d -> p c (h d)"), ps[:, :, 0:192], ACT.Copy).then_inc(sq_ready, 1)
                    freed(st, act.activation(V[:, 2 * k:2 * k + 2, 0:64], ps[:, :, 192:256], ACT.Copy), grp)
                elif kind == "qt":
                    freed(st, act.activation(QST[:, k, :, :].rearrange("p h q -> p (h q)"), full(act, st, b, grp)[:, :], ACT.Copy), grp)
                else:
                    ps = full(act, st, b, grp)[:, :].rearrange("p (c v k) -> p v c k", c=2, v=KV)
                    freed(st, act.activation(KST[:, :, k * 256:(k + 1) * 256].rearrange("p v (c k) -> p v c k", c=2), ps, ACT.Copy), grp)

            for st in front:
                front_step(st, first, 0, 0)
            act.wait_ge(late_loaded, 16 * len(late_loads))
            for hi, raw, _ in split_weights:
                act.activation(hi, raw, ACT.Copy).then_inc(hi_ready, 1)
            with act.Fori(0, NB) as b:
                for st in steps:
                    kind = st[0]
                    if kind in ("xT", "qkv", "qt", "kt"):
                        front_step(st, gb, b, b + 1)
                    elif kind == "s" and st[2] == 0:
                        u = st[1]
                        j, h = units[u]
                        act.wait_ge(nb_ready, b * NU + (u + 1))
                        if u >= 3:
                            name = ("t", u - 3, pieces(units[u - 3][0])[-1][0])
                            act.wait_ge(filled[gb.slot[name][0]], gb.filled(name, b))
                        for r, (a, n) in enumerate(pieces(j)):
                            ps = full(act, ("s", u, a), b)
                            freed(("s", u, a), act.activation(Pb[:, u % 3, a * P:(a + n) * P], ps[:, 0:n * P], ACT.Exp, scale=scal[:, 2:3],
                                                              bias=nb[:, u % 4:u % 4 + 1], accum_out=sums[:, j % 2, h, r:r + 1]))
                    elif kind == "t" and tindex[st] % 2:
                        copy_transposed(act, st, b)
                    elif kind == "T" and st[2]:
                        j, a = st[1:]
                        if j >= 2:
                            act.wait_ge(av2_done, b * NC + (j - 1))
                        freed(st, act.activation(PTb[:, (2 * j + a) % 4, :, :].rearrange("p k q -> p (k q)"), full(act, st, b)[:, :], ACT.Copy))
                    elif kind == "yT":
                        ps = full(act, st, b)
                        act.activation(yT[:, :], ps[:, :], ACT.Copy)
                        freed(st, act.activation(yhi[:, st[1], :], ps[:, :], ACT.Copy))
                    elif kind == "sl":
                        freed(st, act.activation(sel[:, :], full(act, st, b)[:, :], ACT.Relu, bias=1.0))
                    elif kind == "h":
                        _, f, n = st
                        if n >= 4:
                            act.wait_ge(h_used, (b * 2 + f) * (NT * NM) + (n - 3))
                        if n >= 2:
                            act.wait_ge(lo_ready[n % 2], (b * 2 + f) * (NT * NM // 2) + n // 2)
                        ps = full(act, st, b)
                        act.activation(Hb[:, n % 2, :], ps[:, :], ACT.Relu, bias=b1[:, n:n + 1])
                        freed(st, act.activation(Hhi[:, n % 4, :], ps[:, :], ACT.Relu, bias=b1[:, n:n + 1]))
                    elif kind == "vt":
                        f = st[1]
                        freed(st, act.activation(Fv[:, f * HC:(f + 1) * HC, :].rearrange("p c d -> p (c d)"), full(act, st, b)[:, :], ACT.Copy))
                    elif kind == "S" and st[2] == 0:
                        j = st[1]
                        act.wait_ge(nb2_ready, b * NC + (j + 1))
                        if j >= 3:
                            act.wait_ge(filled[gb.slot[("T", j - 3, 1)][0]], gb.filled(("T", j - 3, 1), b))
                        for a in range(2):
                            ps = full(act, ("S", j, a), b)
                            freed(("S", j, a), act.activation(Pb[:, j % 3, a * 512:(a + 1) * 512], ps[:, :], ACT.Exp, scale=float(SOFT),
                                                              bias=nb[:, j % 4:j % 4 + 1], accum_out=sums[:, j // 4, j % 4, a:a + 1]))

        @block.vector
        def _(dve):
            count, base = [0], [0]

            def step(ins):
                count[0] += 1
                ins.then_inc(dve_step, 1)
                return count[0]

            def settle(n=None):
                dve.wait_ge(dve_step, base[0] + (count[0] if n is None else n))

            def do(ins):
                step(ins)
                settle()

            def rsqrt(n):
                y, u, x = rs[:, 0, 0:n], rs[:, 1, 0:n], rs[:, 3, 0:n]
                k = count[0]
                for ins in rsqrt_steps(dve, y, u, x):
                    settle(k)
                    k = step(ins())
                    yield
                settle(k)

            def stats(src, cs):
                for c in cs:
                    k = step(dve.bn_stats(bst[:, c, :], src[:, c, :]))
                    yield
                settle(k)
                dve.memset(pad[:, :], 0.0)
                for c in cs:
                    k = step(dve.bn_aggr(mv[:, c, :], bst[:, c, :]))
                yield
                settle(k)

            def layernorm(src, dst, cs, ready):
                cs = list(cs)
                yield from stats(src, cs)
                step(dve.tensor_scalar(rs[:, 3, 0:len(cs)], mv[:, cs[0]:cs[-1] + 1, 1], 1e-5, None, ALU.add))
                yield from rsqrt(len(cs))
                for n, c in enumerate(cs):
                    ins = dve.tensor_scalar(dst[:, c, :], src[:, c, :], mv[:, c, 0:1], rs[:, 0, n:n + 1], ALU.subtract, ALU.mult)
                    if n < len(cs) - 1:
                        step(ins)
                    else:
                        ins.then_inc(ready, 1)
                    yield

            def norm_front(seq, stored):
                dve.wait_ge(x_loaded, seq * 16 + 16)
                dve.wait_ge(out_free, stored)
                yield from stats(X, range(NC))
                k = step(dve.tensor_tensor(rs[:, 2, 0:NC], mv[:, :, 0], mv[:, :, 0], ALU.mult))
                yield
                settle(k)
                step(dve.scalar_tensor_tensor(rs[:, 3, 0:NC], rs[:, 2, 0:NC], 1e-6, mv[:, :, 1], ALU.add, ALU.add))
                yield
                yield from rsqrt(NC)
                for c in range(NC):
                    ins = dve.tensor_scalar(xn[:, c, :], X[:, c, :], rs[:, 0, c:c + 1], None, ALU.mult)
                    if c % HC == HC - 1:
                        ins.then_inc(xn_ready, 1)
                    else:
                        step(ins)
                    yield

            def heads_front(seq):
                for r in range(NC // 2):
                    dve.wait_ge(sq_ready, seq * (NC // 2) + (r + 1))
                    k = step(dve.tensor_reduce(rs[:, 3, 12 * r:12 * r + 12], sq[:, 2 * r:2 * r + 2, :].rearrange("p c (h d) -> p (c h) d", d=HD), AX.X, ALU.add))
                    yield
                settle(k)
                step(dve.tensor_scalar(rs[:, 3, 0:48], rs[:, 3, 0:48], 1e-24, None, ALU.max))
                yield
                yield from rsqrt(48)
                for r in range(NC // 2):
                    k = step(dve.tensor_tensor(QN[:, 2 * r:2 * r + 2, :, :], QN[:, 2 * r:2 * r + 2, :, :],
                                               rs[:, 0, 12 * r:12 * r + 12].rearrange("p (c h) -> p c h", c=2).unsqueeze(3)
                                               .broadcast_to([P, 2, 6, HD]), ALU.mult))
                    yield
                settle(k)
                for c in range(NC):
                    parts = ((QN[:, c, 0:NH, :], QS, (0, 1), (2, 3)), (QN[:, c, NH:, :], KS, (0, 2), (1, 3)))
                    for src, dst, his, los in parts:
                        for n in his:
                            k = step(dve.tensor_copy(dst[:, c, :, n, :].bitcast(F32R), src))
                    yield
                    settle(k)
                    for src, dst, his, los in parts:
                        for n in los:
                            ins = dve.tensor_tensor(dst[:, c, :, n, :].bitcast(F32R), src, dst[:, c, :, his[0], :], ALU.subtract)
                            if dst is KS and n == 3:
                                ins.then_inc(split_ready, 1)
                            else:
                                step(ins)
                    yield

            dve.wait_ge(w_loaded, 16 * len(loads))
            for _ in norm_front(0, PRIMED):
                pass
            for _ in heads_front(0):
                pass
            dve.wait_ge(late_loaded, 16 * len(late_loads))
            dve.wait_ge(zeroed, 5)
            do(dve.tensor_scalar(nthr[:, 0:1], nthr[:, 0:1], -1.0, None, ALU.mult))
            for n in range(NT):
                dve.tensor_scalar(maskw[:, n * NM:(n + 1) * NM, :].rearrange("p m (a w) -> p (m a) w", w=LW),
                                  wide_path[:, 32 * n:32 * n + NL].unsqueeze(2).broadcast_to([96, NL, LW]), BIG, None, ALU.mult).then_inc(pre_ready, 1)
            for dst, src in ((path[:, :], wide_path), (causal[:, :], wide_causal), (identb[:, :], ident[:, :])):
                dve.tensor_copy(dst, src).then_inc(pre_ready, 1)
            for n, (dst, rows) in enumerate(((nwT[:, :], 96), (b1[:, :], NT * NM))):
                k = pre.slot[("pre", n)][0]
                dve.wait_ge(filled[k], pre.filled(("pre", n), 0))
                dve.tensor_copy(dst, bank[k][:, 0:rows]).then_inc(pre_ready, 1)
            for n, (hi, raw, lo) in enumerate(split_weights):
                dve.wait_ge(hi_ready, n + 1)
                dve.tensor_tensor(lo, raw, hi.bitcast(F32), ALU.subtract).then_inc(pre_ready, 1)
            dve.wait_ge(pre_ready, PREPARED)
            before_loop = count[0]
            RSTD = RSQRT_STEPS
            FRONT = (2 * NC + 2 + RSTD + NC - 2) + (NC // 2 + 1 + RSTD + NC // 2 + 7 * NC)
            SOFTMAX1 = sum(len(pieces(j)) * NH + len(pieces(j)) for j in range(NC))
            NORMS = 4 * (2 * HC + 1 + RSTD + HC - 1)
            SOFTMAX2 = 5 * NC
            PER = FRONT + SOFTMAX1 + NORMS + SOFTMAX2

            with dve.Fori(0, NB) as b:
                base[0], count[0] = b * PER + before_loop, 0
                weaving = [layernorm(O, O, range(HC, NC), out_ready)]

                def weave(n):
                    for _ in range(n):
                        next(weaving[0], None)

                def finish():
                    for _ in weaving[0]:
                        pass

                for st in steps:
                    if st[0] == "s":
                        u, a = st[1], st[2]
                        j, h = units[u]
                        ps = full(dve, st, b)
                        n = dict(pieces(j))[a]
                        if u >= 4 and a == 0:
                            dve.wait_ge(drained[gb.slot[("s", u - 4, pieces(units[u - 4][0])[-1][0])][0]],
                                        gb.drained(("s", u - 4, pieces(units[u - 4][0])[-1][0]), b))
                        do(dve.tensor_reduce(mx[:, u % 4, a // 4:a // 4 + 1], ps[:, 0:n * P], AX.X, ALU.max))
                        if a == pieces(j)[-1][0]:
                            if a:
                                dve.tensor_scalar(nb[:, u % 4:u % 4 + 1], mx[:, u % 4, 0:1], mx[:, u % 4, 1:2], scal[:, 3:4], ALU.max, ALU.mult)\
                                   .then_inc(nb_ready, 1)
                            else:
                                dve.tensor_scalar(nb[:, u % 4:u % 4 + 1], mx[:, u % 4, 0:1], scal[:, 3:4], None, ALU.mult).then_inc(nb_ready, 1)
                    elif st[0] == "t":
                        if tindex[st] % 2 == 0:
                            copy_transposed(dve, st, b)
                        weave(2 if units[st[1]][0] < HC else 1)
                    elif st[0] == "av" and units[st[1]][1] == NH - 1:
                        j = units[st[1]][0]
                        u = st[1]
                        last = ("s", u, pieces(j)[-1][0])
                        dve.wait_ge(drained[gb.slot[last][0]], gb.drained(last, b))
                        r = rsum[:, j % 2, :]
                        if len(pieces(j)) == 2:
                            do(dve.tensor_tensor(r, sums[:, j % 2, :, 0], sums[:, j % 2, :, 1], ALU.add))
                            do(dve.reciprocal(r, r))
                        else:
                            do(dve.reciprocal(r, sums[:, j % 2, :, 0]))
                        ps = full(dve, ("av", j), b)[:, 0:NH * 96].rearrange("p (h w) -> p h w", w=96)
                        for v in range(KV):
                            ins = dve.tensor_tensor(AO[:, j % 2, 64 * v:64 * v + 64].rearrange("p (h d) -> p h d", d=HD),
                                                    ps[:, 2 * v:2 * v + 2, HD * v:HD * v + HD],
                                                    r[:, 2 * v:2 * v + 2].unsqueeze(2).broadcast_to([P, 2, HD]), ALU.mult)
                        freed(("av", j), ins)
                    elif st[0] == "at":
                        j = st[1]
                        ps = full(dve, st, b)
                        freed(st, dve.tensor_copy(AOT[:, j * P:(j + 1) * P], ps[:, 0:P]))
                    elif st[0] == "wo":
                        a = st[1]
                        finish()
                        ps = full(dve, st, b)[:, :].rearrange("p (c d) -> p c d", d=D)
                        cs = slice(a * HC, (a + 1) * HC)
                        freed(st, dve.scalar_tensor_tensor(Y[:, cs, :], ps, scal[:, 0:1], X[:, cs, :], ALU.mult, ALU.add))
                        evacuated(dve, st, b)
                        dve.tensor_tensor(Y[:, cs, :], Y[:, cs, :], X[:, cs, :], ALU.add).then_inc(x_used, 1)
                        dve.wait_ge(x_used, b * 2 + (a + 1 + PRIMED))
                        weaving[0] = layernorm(Y, Y, range(a * HC, (a + 1) * HC), y_ready)
                    elif st[0] == "yT" and st[1] == 0:
                        finish()
                    elif st[0] == "nd":
                        f = st[1]
                        evacuated(dve, ("yT", f), b)
                        dve.tensor_tensor(ylo[:, f, :], yT[:, :], yhi[:, f, :].bitcast(F32), ALU.subtract).then_inc(y_lo_ready, 1)
                        ps = full(dve, st, b)
                        freed(st, dve.tensor_scalar(Dm[:, f, :], ps[0:96, :], nthr[:, 0:1], nthr[:, 1:2], ALU.is_ge, ALU.subtract))
                    elif st[0] == "h":
                        if st[1:] == (0, 0):
                            weaving[0] = chain(weaving[0], norm_front(b + 1, b + PRIMED))
                        weave(2)
                        if st[2] % 2 == 0:
                            hidden_low_part(dve, st[1], st[2], b)
                        weave(2)
                    elif st[0] == "o" and st[2] % NM == NM - 1:
                        f, k = st[1], st[2] // NM
                        ps = full(dve, ("o", f, k), b)
                        dst = F[:, k, f * 512:(f + 1) * 512] if k < 2 else FvT[:, :]
                        freed(("o", f, k), dve.tensor_copy(dst, ps[:, :]))
                    elif st == ("xT", 0):
                        finish()
                    elif st == ("qkv", NC // 2 - 1):
                        weaving[0] = heads_front(b + 1)
                    elif st == ("qt", 0):
                        finish()
                    elif st[0] == "S":
                        j, a = st[1:]
                        if j == 0 and a == 0:
                            weaving[0] = iter(())
                        ps = full(dve, st, b)
                        if a == 0 and j >= 4:
                            evacuated(dve, ("S", j - 4, 1), b)
                        k = step(dve.tensor_reduce(mx[:, j % 4, a:a + 1], ps[:, :], AX.X, ALU.max))
                        if a:
                            weave(1)
                            settle(k)
                            do(dve.tensor_scalar(mx[:, j % 4, 0:1], mx[:, j % 4, 0:1], mx[:, j % 4, 1:2], None, ALU.max))
                            dve.tensor_scalar(nb[:, j % 4:j % 4 + 1], mx[:, j % 4, 0:1], -float(SOFT), None, ALU.mult).then_inc(nb2_ready, 1)
                    elif st[0] == "T":
                        j, a = st[1:]
                        if a == 0:
                            if j >= 2:
                                dve.wait_ge(av2_done, b * NC + (j - 1))
                            ps = full(dve, st, b)
                            freed(st, dve.tensor_copy(PTb[:, (2 * j + a) % 4, :, :].rearrange("p k q -> p (k q)"), ps[:, :]))
                        weave(4)
                    elif st[0] == "A":
                        j = st[1]
                        evacuated(dve, ("S", j, 1), b)
                        r = rsum[:, j % 2, 0:1]
                        do(dve.tensor_tensor(r, sums[:, j // 4, j % 4, 0:1], sums[:, j // 4, j % 4, 1:2], ALU.add))
                        do(dve.reciprocal(r, r))
                        ps = full(dve, st, b)
                        freed(st, dve.scalar_tensor_tensor(O[:, j, :], ps[:, 0:D], r, Y[:, j, :], ALU.mult, ALU.add))
                        if j == HC - 1:
                            evacuated(dve, st, b)
                            weaving[0] = layernorm(O, O, range(HC), out_ready)
                finish()
                evacuated(dve, ("A", NC - 1), b)
                assert count[0] == PER, (count[0], PER)
            base[0], count[0] = NB * PER + before_loop, 0
            for _ in layernorm(O, O, range(HC, NC), out_ready):
                pass

        @block.tensor
        def _(pe):
            pe.wait_ge(w_loaded, 16 * len(loads))

            def take(name, b, grp=gb):
                k = grp.slot[name][0]
                pe.wait_ge(drained[k], grp.free(name, b))
                return bank[k]

            def fill(name, ins, grp=gb):
                ins.then_inc(filled[grp.slot[name][0]], 1)

            def front_step(st, grp, b, seq):
                kind, k = st
                if kind == "xT":
                    pe.wait_ge(xn_ready, seq * 2 + (k + 1))
                    ps = take(st, b, grp)
                    for c in range(HC):
                        ins = pe.transpose(ps[:, c * P:(c + 1) * P], xn[:, k * HC + c, :], ident[:, :])
                elif kind == "qkv":
                    evacuated(pe, ("xT", k // 2), b, grp)
                    ps = take(st, b, grp)
                    for c in range(2):
                        ins = pe.matmul(ps[:, c * 256:(c + 1) * 256], hT[:, (2 * k + c) * P:(2 * k + c + 1) * P], wqkv[:, :], start=True, stop=True)
                elif kind == "qt":
                    pe.wait_ge(split_ready, seq * NC + (k + 1))
                    ps = take(st, b, grp)
                    for h in range(NH):
                        ins = pe.transpose(ps[:, h * P:(h + 1) * P], QS[:, k, h, :, :].rearrange("p a d -> p (a d)"), ident[:, :])
                else:
                    ps = take(st, b, grp)
                    for c in range(2):
                        for v in range(KV):
                            ins = pe.transpose(ps[:, (2 * c + v) * P:(2 * c + v + 1) * P], KS[:, 2 * k + c, v, :, :].rearrange("p a d -> p (a d)"), ident[:, :])
                fill(st, ins, grp)

            def front_done(grp, b):
                evacuated(pe, ("kt", NC // 2 - 1), b, grp)

            for st in front:
                front_step(st, first, 0, 0)
            front_done(first, 0)
            pe.wait_ge(late_loaded, 16 * len(late_loads))
            pe.wait_ge(zeroed, 5)
            for n, (src, rows) in enumerate(((nwraw, 96), (b1raw, NT * NM))):
                ps = take(("pre", n), 0, pre)
                fill(("pre", n), pe.transpose(ps[:, 0:rows], src[:, :], ident[0:rows, 0:rows]), pre)
            pe.wait_ge(pre_ready, PREPARED)
            with pe.Fori(0, NB) as b:

                def ready(name):
                    evacuated(pe, name, b)

                for st in steps:
                    if st[0] == "s":
                        u, a = st[1], st[2]
                        j, h = units[u]
                        n = dict(pieces(j))[a]
                        ps = take(st, b)
                        diag = a + n - 1 == j
                        ins = pe.matmul(ps[:, 0:n * P], QST[:, j, h, :], KST[:, h // 2, a * P:(a + n) * P], start=True, stop=not diag, skip_group_check=True)
                        if diag:
                            ins = pe.matmul(ps[:, (n - 1) * P:n * P], identb[:, :], causal[:, :], start=False, stop=True, skip_group_check=True)
                        fill(st, ins)
                    elif st[0] == "t":
                        u, a = st[1], st[2]
                        ready(("s", u, a))
                        ps = take(st, b)
                        for k in range(dict(pieces(units[u][0]))[a]):
                            ins = pe.transpose(ps[:, k * P:(k + 1) * P], Pb[:, u % 3, (a + k) * P:(a + k + 1) * P], ident[:, :])
                        fill(st, ins)
                    elif st[0] == "av":
                        u = st[1]
                        j, h = units[u]
                        ps = take(("av", j), b) if h == 0 else bank[gb.slot[("av", j)][0]]
                        for a, n in pieces(j):
                            ready(("t", u, a))
                            for k in range(n):
                                ins = pe.matmul(ps[:, h * 96:(h + 1) * 96], PT_places[tindex[("t", u, a)] % len(PT_places)][:, k * P:(k + 1) * P], V[:, a + k, :],
                                                start=(a + k == 0), stop=(a + k == j), skip_group_check=True)
                        ins.then_inc(av_done, 1)
                        if h == NH - 1:
                            pe.wait_ge(av_done, b * NU + (u + 1))
                            pe.nop().then_inc(filled[gb.slot[("av", j)][0]], 1)
                    elif st[0] == "at":
                        j = st[1]
                        ready(("av", j))
                        ps = take(st, b)
                        fill(st, pe.transpose(ps[:, 0:P], AO[:, j % 2, :], ident[:, :]))
                    elif st[0] in ("xT", "qkv", "qt", "kt"):
                        front_step(st, gb, b, b + 1)
                    elif st[0] == "wo":
                        a = st[1]
                        ready(("at", (a + 1) * HC - 1))
                        ps = take(st, b)
                        for c in range(HC):
                            ins = pe.matmul(ps[:, c * P:(c + 1) * P], AOT[:, (a * HC + c) * P:(a * HC + c + 1) * P], wo[:, :], start=True, stop=True)
                        fill(st, ins)
                    elif st[0] == "yT":
                        f = st[1]
                        pe.wait_ge(y_ready, b * 2 + (f + 1))
                        ps = take(st, b)
                        for c in range(HC):
                            ins = pe.transpose(ps[:, c * P:(c + 1) * P], Y[:, f * HC + c, :], ident[:, :])
                        fill(st, ins)
                    elif st[0] == "nd":
                        f = st[1]
                        ready(("yT", f))
                        ps = take(st, b)
                        fill(st, pe.matmul(ps[0:96, :], nwT[:, :], yT[:, :], start=True, stop=True))
                    elif st[0] == "sl":
                        f = st[1]
                        if f == 1:
                            ready(("nd", f))
                        ps = take(st, b)
                        fill(st, pe.matmul(ps[:, :], path[:, :], Dm[:, f, :], start=True, stop=True))
                    elif st[0] == "h":
                        _, f, n = st
                        k, m = n // NM, n % NM
                        ps = take(st, b)
                        if n == 0:
                            pe.wait_ge(y_lo_ready, b * 2 + (f + 1))
                        cols = slice(m * P, (m + 1) * P)
                        pe.matmul(ps[:, :], W1hi[:, k, cols], yhi[:, f, :], start=True, stop=False)
                        pe.matmul(ps[:, :], W1lo[:, k, cols], yhi[:, f, :], start=False, stop=False)
                        pe.matmul(ps[:, :], W1hi[:, k, cols], ylo[:, f, :], start=False, stop=False)
                        if (f, n) == (0, 0):
                            ready(("nd", f))
                        fill(st, pe.matmul(ps[:, :], maskw[:, n, :], Dm[:, f, :], start=False, stop=True))
                    elif st[0] == "o":
                        _, f, n = st
                        k, m = n // NM, n % NM
                        if m == 0:
                            ready(("sl", f))
                            ps = take(("o", f, k), b)
                            pe.matmul(ps[:, :], b2hi[:, k, :], sel[:, :], start=True, stop=False)
                            pe.matmul(ps[:, :], b2lo[:, k, :], sel[:, :], start=False, stop=False)
                        ps = bank[gb.slot[("o", f, k)][0]]
                        ready(("h", f, n))
                        pe.matmul(ps[:, :], W2hi[:, k, m, :], Hhi[:, n % 4, :], start=False, stop=False)
                        pe.matmul(ps[:, :], W2lo[:, k, m, :], Hhi[:, n % 4, :], start=False, stop=False)
                        pe.wait_ge(lo_ready[n % 2], (b * 2 + f) * (NT * NM // 2) + (n // 2 + 1))
                        ins = pe.matmul(ps[:, :], W2hi[:, k, m, :], Hlo[:, n % 4, :], start=False, stop=(m == NM - 1))
                        ins.then_inc(h_used, 1)
                        if m == NM - 1:
                            pe.wait_ge(h_used, (b * 2 + f) * (NT * NM) + (n + 1))
                            pe.nop().then_inc(filled[gb.slot[("o", f, k)][0]], 1)
                    elif st[0] == "vt":
                        f = st[1]
                        ready(("o", f, 2))
                        ps = take(st, b)
                        for c in range(HC):
                            ins = pe.transpose(ps[:, c * P:(c + 1) * P], FvT[:, c * P:(c + 1) * P], ident[:, :])
                        fill(st, ins)
                    elif st[0] == "S":
                        _, j, a = st
                        if j == 0:
                            ready(("o", a, 1))
                        ps = take(st, b)
                        fill(st, pe.matmul(ps[:, :], F[:, 0, j * P:(j + 1) * P], F[:, 1, a * 512:(a + 1) * 512], start=True, stop=True))
                    elif st[0] == "T":
                        _, j, a = st
                        ready(("S", j, a))
                        ps = take(st, b)
                        for k in range(4):
                            ins = pe.transpose(ps[:, k * P:(k + 1) * P], Pb[:, j % 3, (4 * a + k) * P:(4 * a + k + 1) * P], ident[:, :])
                        fill(st, ins)
                    elif st[0] == "A":
                        j = st[1]
                        if j == 0:
                            ready(("vt", 1))
                        ps = take(st, b)
                        for a in range(2):
                            ready(("T", j, a))
                            for k in range(4):
                                ins = pe.matmul(ps[:, 0:D], PTb[:, (2 * j + a) % 4, k, :], Fv[:, 4 * a + k, :], start=(a + k == 0), stop=(4 * a + k == NC - 1))
                        ins.then_inc(av2_done, 1)
                        pe.wait_ge(av2_done, b * NC + (j + 1))
                        pe.nop().then_inc(filled[gb.slot[st][0]], 1)
                front_done(gb, b)


def tree_constants(trees=3, depth=4):
    nodes, leaves = 2 ** depth - 1, 2 ** depth
    path = np.zeros((96, P), np.float32)
    for k in range(trees):
        for leaf in range(leaves):
            cur = leaf + nodes
            while cur:
                parent, right = (cur - 1) // 2, (cur - 1) % 2
                if right:
                    path[32 * k + nodes + parent, 32 * k + leaf] = 1.0
                else:
                    path[32 * k + parent, 32 * k + leaf] = -1.0
                cur = parent
    comp = np.zeros((96, 1), np.float32)
    for k in range(trees):
        comp[32 * k + nodes:32 * k + 2 * nodes] = 1.0
    return {"c_path": path, "c_comp": comp, "c_causal": np.triu(np.full((P, P), -BIG, np.float32), 1)}


def kernel(**inputs):
    import concourse.bacc as bacc
    from concourse.bass_utils import run_bass_kernel_spmd as run

    nc = bacc.Bacc("TRN2", target_bir_lowering=False, num_devices=1)
    arrays = {name: np.ascontiguousarray(a) for name, a in inputs.items()}
    arrays["c_ident"] = np.eye(P, dtype=np.float32)
    arrays["c_mask"] = np.triu(np.ones((P, P), np.float32))
    arrays.update(tree_constants())
    t = {}
    for name, a in arrays.items():
        t[name] = nc.dram_tensor(name, a.shape, mybir.dt.from_np(a.dtype), kind="ExternalInput").ap()
    shape = arrays["L0_attn_x"].shape
    t["out"] = nc.dram_tensor("out", shape, F32, kind="ExternalOutput").ap()
    t["x_mid"] = nc.dram_tensor("x_mid", (shape[0] * shape[1] // (4 * P) + 1, P, 4 * shape[2]), F32, kind="Internal").ap()
    build(nc, t)
    return run(nc, [arrays], core_ids=[0]).results[0]["out"]
```
